# Optimizing a Trainium2 kernel written in Bass

```python
import numpy as np
import jax
import jax.numpy as jnp

def _softmax(x, axis=-1):
    return jax.nn.softmax(x, axis=axis)

def _gelu(x):
    return jax.nn.gelu(x, approximate=True)

def _silu(x):
    return jax.nn.silu(x)

def _sigmoid(x):
    return jax.nn.sigmoid(x)

def _layernorm(x, axis=-1, eps=1e-05):
    m = jnp.mean(x, axis=axis, keepdims=True)
    v = jnp.var(x, axis=axis, keepdims=True)
    return (x - m) / jnp.sqrt(v + eps)

def _scatter_add(tgt, idx, src, axis=0):
    return tgt.at[idx].add(src)

def _segment_sum(src, seg, n):
    return jax.ops.segment_sum(src, seg, n)
kernel_name = 'mk_xattn_ffn_d1_seqx_r4_d66062'

def setup_inputs(seed: int=0):
    np.random.seed(seed)
    _w = jnp.asarray

    def _rec_inputs():
        import jax
        import jax.numpy as jnp
        _rk = jax.random.key(seed)
        x = 4.136e-05 + 0.9999 * jax.random.normal(jax.random.fold_in(_rk, 1), (4, 512, 512), jnp.float32)
        _lenS = 512 - jax.random.randint(jax.random.fold_in(_rk, 7), (4,), 0, max(1, 512 // 4) + 1, jnp.int32)
        _lenS2 = 512 - jax.random.randint(jax.random.fold_in(_rk, 8), (4,), 0, max(1, 512 // 4) + 1, jnp.int32)
        _ctx_1024P = jax.random.normal(jax.random.fold_in(_rk, 11), (4, 16, 256), jnp.float32)
        _ctx_1024c = jax.random.dirichlet(jax.random.fold_in(_rk, 511), 0.3 * jnp.ones((16,), jnp.float32), (4, 512))
        _ctx_1024t = jnp.einsum('bsk,bkd->bsd', _ctx_1024c, _ctx_1024P)
        _ctx_1024t = _ctx_1024t * jax.lax.rsqrt(jnp.mean(jnp.square(_ctx_1024t)) + 1e-12) * 0.953939
        ctx_1024 = -0.000292821 + 1.00034 * (_ctx_1024t + 0.3 * jax.random.normal(jax.random.fold_in(_rk, 611), (4, 512, 256), jnp.float32))
        return (x, ctx_1024)
    x, ctx_1024 = _rec_inputs()

    def _L0_xattn_setup():
        import jax, jax.numpy as jnp
        import numpy as np
        import math
        B, L, DM = (2, 512, 256)
        DS, DC, EXP = (16, 4, 2)
        DI = EXP * DM
        DR = math.ceil(DM / 16)
        DT_MIN, DT_MAX, DT_FLOOR = (0.001, 0.1, 0.0001)

        def _ssm_forward(hidden_states, z, in_proj_w, conv_w, conv_b, x_proj_w, dt_proj_w, dt_proj_b, A_log, D):
            b = hidden_states.shape[0]
            x = jnp.einsum('ed,bld->bel', in_proj_w, hidden_states)
            xp = jnp.pad(x, ((0, 0), (0, 0), (DC - 1, 0)))
            xc = jax.lax.conv_general_dilated(xp, conv_w[:, None, :], window_strides=(1,), padding='VALID', dimension_numbers=('NCH', 'OIH', 'NCH'), feature_group_count=DI)
            u = jax.nn.silu(xc + conv_b[None, :, None])
            x_dbl = jnp.einsum('ke,bel->bkl', x_proj_w, u)
            dt_lo = x_dbl[:, :DR]
            Bm = x_dbl[:, DR:DR + DS]
            Cm = x_dbl[:, DR + DS:]
            delta = jax.nn.softplus(jnp.einsum('er,brl->bel', dt_proj_w, dt_lo) + dt_proj_b[None, :, None])
            A = -jnp.exp(A_log)

            def step(state, xs):
                d_t, B_t, C_t, u_t = xs
                dA = jnp.exp(d_t[..., None] * A)
                state = state * dA + (d_t * u_t)[..., None] * B_t[:, None, :]
                y_t = jnp.einsum('ben,bn->be', state, C_t)
                return (state, y_t)
            xs = (jnp.moveaxis(delta, -1, 0), jnp.moveaxis(Bm, -1, 0), jnp.moveaxis(Cm, -1, 0), jnp.moveaxis(u, -1, 0))
            state0 = jnp.zeros((b, DI, DS), delta.dtype)
            _, ys = jax.lax.scan(step, state0, xs)
            y = jnp.moveaxis(ys, 0, -1)
            y = y + D[None, :, None] * u
            y = y * jax.nn.silu(z)
            return jnp.swapaxes(y, 1, 2)
        key = jax.random.key(seed)
        ks = jax.random.split(key, 8)
        hidden_states = jax.random.normal(ks[0], (B, L, DM), jnp.float32)
        z = jax.random.normal(ks[1], (B, DI, L), jnp.float32)
        in_proj_w = jax.random.normal(ks[2], (DI, DM), jnp.float32) * DM ** (-0.5)
        conv_w = jax.random.normal(ks[3], (DI, DC), jnp.float32) * DC ** (-0.5)
        conv_b = jnp.zeros((DI,), jnp.float32)
        x_proj_w = jax.random.normal(ks[4], (DR + 2 * DS, DI), jnp.float32) * DI ** (-0.5)
        dt_std = DR ** (-0.5)
        dt_proj_w = jax.random.uniform(ks[5], (DI, DR), jnp.float32, -dt_std, dt_std)
        dt = jnp.exp(jax.random.uniform(ks[6], (DI,), jnp.float32) * (math.log(DT_MAX) - math.log(DT_MIN)) + math.log(DT_MIN))
        dt = jnp.clip(dt, DT_FLOOR)
        dt_proj_b = dt + jnp.log(-jnp.expm1(-dt))
        A_log = jnp.log(jnp.broadcast_to(jnp.arange(1, DS + 1, dtype=jnp.float32), (DI, DS)))
        D = jnp.ones((DI,), jnp.float32)
        return dict(hidden_states=hidden_states, z=z, in_proj_w=in_proj_w, conv_w=conv_w, conv_b=conv_b, x_proj_w=x_proj_w, dt_proj_w=dt_proj_w, dt_proj_b=dt_proj_b, A_log=A_log, D=D)
    _L0_xattn_all = _L0_xattn_setup()
    _L0_xattn_in = {k: v for k, v in _L0_xattn_all.items() if k in ('in_proj_w', 'conv_w', 'conv_b', 'x_proj_w', 'dt_proj_w', 'dt_proj_b', 'A_log', 'D')}
    del _L0_xattn_all

    def _L0_ffn_setup():
        import jax, jax.numpy as jnp
        import numpy as np
        HIDDEN = 512
        INTER = 1376
        LUT_SIZE = 16

        def _ghost_linear(x, idx, lut):
            w = lut[idx]
            return jnp.einsum('bsh,oh->bso', x, w)
        key = jax.random.key(seed)
        k_x, k_lut, k_g, k_u, k_d = jax.random.split(key, 5)
        x = jax.random.normal(k_x, (2, 1024, HIDDEN), dtype=jnp.float32)
        lut = jax.random.normal(k_lut, (LUT_SIZE,), dtype=jnp.float32) * 0.02
        gate_idx = jax.random.randint(k_g, (INTER, HIDDEN), 0, LUT_SIZE, dtype=jnp.int32)
        up_idx = jax.random.randint(k_u, (INTER, HIDDEN), 0, LUT_SIZE, dtype=jnp.int32)
        down_idx = jax.random.randint(k_d, (HIDDEN, INTER), 0, LUT_SIZE, dtype=jnp.int32)
        return {'x': x, 'lut': lut, 'gate_idx': gate_idx, 'up_idx': up_idx, 'down_idx': down_idx}
    _L0_ffn_all = _L0_ffn_setup()
    _L0_ffn_in = {k: v for k, v in _L0_ffn_all.items() if k in ('lut', 'gate_idx', 'up_idx', 'down_idx')}
    del _L0_ffn_all
    return {'x': x, 'ctx_1024': ctx_1024, 'L0_xattn_in_proj_w': _L0_xattn_in['in_proj_w'], 'L0_xattn_conv_w': _L0_xattn_in['conv_w'], 'L0_xattn_conv_b': _L0_xattn_in['conv_b'], 'L0_xattn_x_proj_w': _L0_xattn_in['x_proj_w'], 'L0_xattn_dt_proj_w': _L0_xattn_in['dt_proj_w'], 'L0_xattn_dt_proj_b': _L0_xattn_in['dt_proj_b'], 'L0_xattn_A_log': _L0_xattn_in['A_log'], 'L0_xattn_D': _L0_xattn_in['D'], 'L0_ffn_lut': _L0_ffn_in['lut'], 'L0_ffn_gate_idx': _L0_ffn_in['gate_idx'], 'L0_ffn_up_idx': _L0_ffn_in['up_idx'], 'L0_ffn_down_idx': _L0_ffn_in['down_idx']}

def reference(x, ctx_1024, L0_xattn_in_proj_w, L0_xattn_conv_w, L0_xattn_conv_b, L0_xattn_x_proj_w, L0_xattn_dt_proj_w, L0_xattn_dt_proj_b, L0_xattn_A_log, L0_xattn_D, L0_ffn_lut, L0_ffn_gate_idx, L0_ffn_up_idx, L0_ffn_down_idx):
    import jax
    import jax.numpy as jnp

    def _L0_xattn_ref(hidden_states, z, in_proj_w, conv_w, conv_b, x_proj_w, dt_proj_w, dt_proj_b, A_log, D):
        import jax, jax.numpy as jnp
        import numpy as np
        import math
        B, L, DM = (2, 512, 256)
        DS, DC, EXP = (16, 4, 2)
        DI = EXP * DM
        DR = math.ceil(DM / 16)
        DT_MIN, DT_MAX, DT_FLOOR = (0.001, 0.1, 0.0001)

        def _ssm_forward(hidden_states, z, in_proj_w, conv_w, conv_b, x_proj_w, dt_proj_w, dt_proj_b, A_log, D):
            b = hidden_states.shape[0]
            x = jnp.einsum('ed,bld->bel', in_proj_w, hidden_states)
            xp = jnp.pad(x, ((0, 0), (0, 0), (DC - 1, 0)))
            xc = jax.lax.conv_general_dilated(xp, conv_w[:, None, :], window_strides=(1,), padding='VALID', dimension_numbers=('NCH', 'OIH', 'NCH'), feature_group_count=DI)
            u = jax.nn.silu(xc + conv_b[None, :, None])
            x_dbl = jnp.einsum('ke,bel->bkl', x_proj_w, u)
            dt_lo = x_dbl[:, :DR]
            Bm = x_dbl[:, DR:DR + DS]
            Cm = x_dbl[:, DR + DS:]
            delta = jax.nn.softplus(jnp.einsum('er,brl->bel', dt_proj_w, dt_lo) + dt_proj_b[None, :, None])
            A = -jnp.exp(A_log)

            def step(state, xs):
                d_t, B_t, C_t, u_t = xs
                dA = jnp.exp(d_t[..., None] * A)
                state = state * dA + (d_t * u_t)[..., None] * B_t[:, None, :]
                y_t = jnp.einsum('ben,bn->be', state, C_t)
                return (state, y_t)
            xs = (jnp.moveaxis(delta, -1, 0), jnp.moveaxis(Bm, -1, 0), jnp.moveaxis(Cm, -1, 0), jnp.moveaxis(u, -1, 0))
            state0 = jnp.zeros((b, DI, DS), delta.dtype)
            _, ys = jax.lax.scan(step, state0, xs)
            y = jnp.moveaxis(ys, 0, -1)
            y = y + D[None, :, None] * u
            y = y * jax.nn.silu(z)
            return jnp.swapaxes(y, 1, 2)
        return _ssm_forward(hidden_states, z, in_proj_w, conv_w, conv_b, x_proj_w, dt_proj_w, dt_proj_b, A_log, D)

    def _L0_ffn_ref(x, lut, gate_idx, up_idx, down_idx):
        import jax, jax.numpy as jnp
        import numpy as np
        HIDDEN = 512
        INTER = 1376
        LUT_SIZE = 16

        def _ghost_linear(x, idx, lut):
            w = lut[idx]
            return jnp.einsum('bsh,oh->bso', x, w)
        gate = _ghost_linear(x, gate_idx, lut)
        up = _ghost_linear(x, up_idx, lut)
        h = jax.nn.silu(gate) * up
        return _ghost_linear(h, down_idx, lut)
    x = x + _L0_xattn_ref(ctx_1024, _layernorm(x, axis=-1), L0_xattn_in_proj_w, L0_xattn_conv_w, L0_xattn_conv_b, L0_xattn_x_proj_w, L0_xattn_dt_proj_w, L0_xattn_dt_proj_b, L0_xattn_A_log, L0_xattn_D)
    x = x + _L0_ffn_ref(_layernorm(x, axis=-1), L0_ffn_lut, L0_ffn_gate_idx, L0_ffn_up_idx, L0_ffn_down_idx)
    return x

_drawn_inputs = setup_inputs


def setup_inputs(seed=0):
    import zlib

    import numpy as np

    out = dict(_drawn_inputs(seed))
    spreads = {'L0_xattn_conv_b': (0.0, 0.1), 'L0_xattn_D': (1.0, 0.2)}
    factors = {'L0_xattn_dt_proj_w': 5.222}
    for name, (base, spread) in spreads.items():
        noise = np.random.default_rng([zlib.crc32(name.encode()), seed]).standard_normal(out[name].shape)
        drawn = base * np.exp(spread * noise) if base else spread * noise
        out[name] = jnp.asarray(drawn.astype(out[name].dtype))
    for name, factor in factors.items():
        out[name] = (out[name] * factor).astype(out[name].dtype)
    return out
```

```python
from contextlib import ExitStack

import concourse.bass as bass
import concourse.mybir as mybir

ALU = mybir.AluOpType
ACT = mybir.ActivationFunctionType
AX = mybir.AxisListType
F32 = mybir.dt.float32
F16 = mybir.dt.float16
I32 = mybir.dt.int32

P = 128
EPS = 1e-5


def after(eng, sem, count):
    if isinstance(count, int) and count <= 0:
        return
    eng.wait_ge(sem, count)


def settled(eng, sem):
    eng.sem_inc(sem, 1)


def mamba_ffn(nc, ctx_t, x, win_t, conv_w, conv_b, xproj_t, dt_t, dt_b, a_log, d_skip, lut, idx, out):
    NB, DM, L = ctx_t.shape
    DI = win_t.shape[1]
    DS = a_log.shape[1]
    DR = dt_t.shape[0]
    KC = conv_w.shape[1]
    NX = xproj_t.shape[1]
    NLUT = lut.shape[0]
    HID = x.shape[2]
    F = idx.shape[1]
    INTER = 1376
    KT = HID // P
    ET = DI // P
    KM = DM // P
    LT = L // P
    JT = -(-INTER // P)
    TC = 256
    CT = TC // P
    NCH = NB * L // TC
    UP0 = KT * INTER
    DN0 = 2 * KT * INTER
    PIECES = 8
    PW = F // (NB * PIECES)
    ACT_AFF = 4
    NPAIR = NLUT // 2
    GR = 4
    NG = DS // GR
    assert F == NB * PIECES * PW and F == DN0 + JT * HID and L == CT * P * 2
    assert NX == DR + 2 * DS

    def rows(j):
        return min(P, INTER - j * P)

    def dram(name, shape):
        return nc.dram_tensor(name, shape, F32, kind="Internal").ap()

    dd_d = dram("dd_scratch", [NCH, P, 2, ET, TC])
    b_d = dram("b_scratch", [NCH, DS, TC])
    ct_d = dram("ct_scratch", [NCH, P, CT, DS])
    ud_d = dram("ud_scratch", [NCH, CT, P, DI])
    gz_d = dram("gz_scratch", [NCH, CT, P, L])

    ctx = ExitStack()
    with ctx:
        def sem(name):
            return ctx.enter_context(nc.semaphore(name))

        def sb(name, shape, dt=F32):
            return ctx.enter_context(nc.sbuf_tensor(name, shape, dt))

        bank = [ctx.enter_context(nc.psum_tensor(f"bank{i}", [P, 512], F32)) for i in range(8)]

        w_hi = sb("w_hi", [P, F], F16)
        w_lo = sb("w_lo", [P, F], F16)
        ident = sb("ident", [P, P])
        neg_a = sb("neg_a", [P, ET, DS])
        sc = sb("sc", [P, 8])
        lut_s = sb("lut_s", [P, NLUT])
        lut_d = sb("lut_d", [P, NPAIR])
        half = sb("half", [P, LT])
        out_scale, tanh_scale = sc[:, 0:1], sc[:, 1:2]

        ctxA = ExitStack()

        def sa(name, shape, dt=F32):
            return ctxA.enter_context(nc.sbuf_tensor(name, shape, dt))

        ctx_sb = sa("ctx_sb", [P, KM, L])
        x_sb = sa("x_sb", [P, LT, HID])
        win_sb = sa("win_sb", [P, KM, DI])
        xproj_sb = sa("xproj_sb", [P, ET, NX])
        dt_sb = sa("dt_sb", [DR, DI])
        xdbl_sb = sa("xdbl_sb", [NX, L])
        conv_diag = sa("conv_diag", [P, ET, KC, P])
        d_diag = sa("d_diag", [P, ET, P])
        cw_sb = sa("cw_sb", [P, ET, KC])
        vec = sa("vec", [P, 3, ET])
        cb_half = sa("cb_half", [P, ET])
        xpad = sa("xpad", [P, 2, L + KC - 1])
        v_half = sa("v_half", [P, 2, L])
        v_tanh = sa("v_tanh", [P, 2, L])
        u_sb = sa("u_sb", [P, ET, L])
        e_abs = sa("e_abs", [P, 2, L])
        e_exp = sa("e_exp", [P, ET, L])
        e_ln = sa("e_ln", [P, ET, L])
        e_relu = sa("e_relu", [P, ET, L])
        delta_st = sa("delta_st", [P, 2, L])
        du_st = sa("du_st", [P, 2, L])
        ud_st = sa("ud_st", [P, 2, DI])
        gz_st = sa("gz_st", [P, 2, LT, P])
        ct_st = sa("ct_st", [P, LT, DS])
        zn = sa("zn", [P, LT, HID])
        z_tanh = sa("z_tanh", [P, 2, HID])
        stats = sa("stats", [P, LT, 6])
        mv = sa("mv", [P, LT, 2])
        zsc = sa("zsc", [P, 4, LT])
        idx_sb = sa("idx_sb", [P, 2, PW], I32)
        bit0 = sa("bit0", [P, 2, PW], I32)
        bits = sa("bits", [P, 3, PW], I32)
        pair = sa("pair", [P, NPAIR, PW])
        lut_in = sa("lut_in", [P, NLUT])
        lut_i = sa("lut_i", [P, 4], I32)
        ctxA.close()

        ctxB = ctx.enter_context(ExitStack())

        def sB(name, shape, dt=F32):
            return ctxB.enter_context(nc.sbuf_tensor(name, shape, dt))

        dd = sB("dd", [P, 2, 2, ET, TC])
        b_rows = sB("b_rows", [P, 2, GR, TC])
        ct = sB("ct", [P, 2, CT, DS])
        db = sB("db", [P, 2, ET, TC])
        h = sB("h", [P, 2, ET, TC])
        h_last = sB("h_last", [P, DS, ET])
        init = sB("init", [P, CT, DI])
        acc = sB("acc", [P, CT, DI])
        gz = sB("gz", [P, CT, DI])
        x_in = sB("x_in", [P, CT, HID])
        x1 = sB("x1", [P, 2, CT, HID])
        xn = sB("xn", [P, CT, HID])
        xt_hi = sB("xt_hi", [P, KT, TC], F16)
        xt_lo = sB("xt_lo", [P, KT, TC], F16)
        g_tanh = sB("g_tanh", [P, 2, TC])
        u_gate = sB("u_gate", [P, 2, 2, TC])
        q_gate = sB("q_gate", [P, 2, 2, TC])
        h_hi = sB("h_hi", [P, JT + 1, TC], F16)
        h_lo = sB("h_lo", [P, JT + 1, TC], F16)
        out_sb = sB("out_sb", [P, CT, HID])
        stats2 = sB("stats2", [P, CT, 6])
        mv2 = sB("mv2", [P, CT, 2])
        nsc = sB("nsc", [P, 4, CT])

        names = """params_loaded lut_loaded vec_loaded ctx_loaded xa_loaded ident_zero ident_ready setup setup_act
            half_ready xp_ready xpad_ready pad_zero v_ready vhalf_ready u_ready xdbl_ready xdbl_sb_ready ud_ready
            ud_free dt_ready eabs_ready erelu_ready eexp_ready w_ready t_ready ln_ready sp_ready delta_ready
            ctt_ready ct_ready zstat zsc_ready zpow zn_ready ztanh_ready gz_ready gzt_ready gz_st_ready
            masks_ready pairs_act pairs_pool level picked whi_ready wlo_ready
            b_stored ct_stored phase_a scan_done exp_done db_done ht_ready stt_done hl_saved b_used
            init_loaded gz_loaded x_loaded x1_ready fin_stat nsc_ready npow xn_ready xnt_ready xhi_ready xlo_ready
            gu_ready gt_ready us_ready q_ready hs_ready hhi_ready hlo_ready dn_ready out_ready
            passed_sp passed_pool passed_dve passed_pe""".split()
        S = {name: sem(name) for name in names}
        idx_loaded = [sem(f"idx_loaded{i}") for i in range(2)]
        delta_stored = [sem(f"delta_stored{i}") for i in range(2)]
        du_stored = [sem(f"du_stored{i}") for i in range(2)]
        ud_stored = [sem(f"ud_stored{i}") for i in range(2)]
        gz_stored = [sem(f"gz_stored{i}") for i in range(2)]
        dd_loaded = [sem(f"dd_loaded{i}") for i in range(2)]
        b_loaded = [sem(f"b_loaded{i}") for i in range(2)]
        out_stored = [sem(f"out_stored{i}") for i in range(CT)]

        block = ctx.enter_context(nc.Block())

        down_parts = [
            [(0, j) for j in range(5)],
            [(0, j) for j in range(5, 8)] + [(1, j) for j in range(3)],
            [(0, j) for j in range(8, JT)] + [(1, j) for j in range(3, 6)],
            [(1, j) for j in range(6, JT)],
        ]
        GU0 = 3

        @block.sync
        def _(sp):
            sp.dma_start(lut_in[:], lut.rearrange("(a n) -> a n", a=1).partition_broadcast(P)
                         .rearrange("p a n -> p (a n)")).then_inc(S["lut_loaded"], 16)
            sp.dma_start(win_sb[:], win_t.rearrange("(k p) e -> p k e", p=P)).then_inc(S["params_loaded"], 16)
            sp.dma_start(cw_sb[:], conv_w.rearrange("(t p) k -> p t k", p=P)).then_inc(S["vec_loaded"], 16)
            with nc.allow_non_contiguous_dma(reason="512 numbers each"):
                for i, v in enumerate((conv_b, dt_b, d_skip)):
                    sp.dma_start(vec[:, i, :], v.rearrange("(t p) -> p t", p=P)).then_inc(S["vec_loaded"], 16)
            sp.dma_start(neg_a[:], a_log.rearrange("(t p) n -> p t n", p=P)).then_inc(S["vec_loaded"], 16)
            sp.dma_start(xproj_sb[:], xproj_t.rearrange("(t p) k -> p t k", p=P)).then_inc(S["params_loaded"], 16)
            sp.dma_start(dt_sb[:], dt_t).then_inc(S["params_loaded"], 16)

            def load_batch(nxt, b=None):
                if b is not None:
                    sp.wait_ge(S["xp_ready"], b * ET + ET)
                    settled(sp, S["passed_sp"])
                sp.dma_start(ctx_sb[:], ctx_t[bass.ds(nxt, 1)].rearrange("a (k p) l -> p (a k) l", p=P))\
                    .then_inc(S["ctx_loaded"], 16)
                if b is not None:
                    sp.wait_ge(S["zn_ready"], b * LT + LT)
                    settled(sp, S["passed_sp"])
                sp.dma_start(x_sb[:], x[bass.ds(nxt, 1)].rearrange("a (s p) h -> p (a s) h", p=P))\
                    .then_inc(S["xa_loaded"], 16)

            load_batch(0)

            def idx_piece(b, s):
                after(sp, S["masks_ready"], b * PIECES + max(s - 1, 0))
                settled(sp, S["passed_sp"])
                sp.dma_start(idx_sb[:, s % 2, :], idx[:, bass.ds(b * (PIECES * PW) + s * PW, PW)])\
                    .then_inc(idx_loaded[s % 2], 16)

            def half_view(d, b, hf):
                return d[bass.ds(b * 2 + hf, 1)]

            def batch(b):
                for s in range(3):
                    idx_piece(b, s)
                load_batch((b + 1) % NB, b)
                idx_piece(b, 3)
                sp.wait_ge(S["xdbl_sb_ready"], b + 1)
                settled(sp, S["passed_sp"])
                for hf in range(2):
                    sp.dma_start(half_view(b_d, b, hf).rearrange("a n t -> n (a t)"),
                                 xdbl_sb[DR:DR + DS, hf * TC:(hf + 1) * TC]).then_inc(S["b_stored"], 16)
                sp.wait_ge(S["ct_ready"], b + 1)
                settled(sp, S["passed_sp"])
                for hf in range(2):
                    sp.dma_start(half_view(ct_d, b, hf).rearrange("a p c n -> p (a c) n"),
                                 ct_st[:, hf * CT:(hf + 1) * CT, :]).then_inc(S["ct_stored"], 16)
                idx_piece(b, 4)
                for st in range(LT):
                    sp.wait_ge(S["gz_st_ready"], b * LT + st + 1)
                    settled(sp, S["passed_sp"])
                    for hf in range(2):
                        sp.dma_start(
                            half_view(gz_d, b, hf)[:, :, :, st * P:(st + 1) * P].rearrange("a c p s -> p (a c) s"),
                            gz_st[:, st % 2, hf * CT:(hf + 1) * CT, :]).then_inc(gz_stored[st % 2], 16)
                idx_piece(b, 5)
                for tt in range(LT):
                    sp.wait_ge(S["ud_free"], b * LT + tt + 1)
                    settled(sp, S["passed_sp"])
                    sp.dma_start(half_view(ud_d, b, tt // CT)[:, tt % CT].rearrange("a p e -> p (a e)"),
                                 ud_st[:, tt % 2, :]).then_inc(ud_stored[tt % 2], 16)
                idx_piece(b, 6)
                idx_piece(b, 7)
                for et in range(ET):
                    sp.wait_ge(S["sp_ready"], b * ET + et + 1)
                    settled(sp, S["passed_sp"])
                    for hf in range(2):
                        dst = half_view(dd_d, b, hf)
                        sp.dma_start(dst[:, :, 0, et, :].rearrange("a p t -> p (a t)"),
                                     delta_st[:, et % 2, hf * TC:(hf + 1) * TC]).then_inc(delta_stored[et % 2], 16)
                        sp.dma_start(dst[:, :, 1, et, :].rearrange("a p t -> p (a t)"),
                                     du_st[:, et % 2, hf * TC:(hf + 1) * TC]).then_inc(du_stored[et % 2], 16)

            batch(0)
            with sp.Fori(1, NB) as b:
                batch(b)

            for i in range(2):
                sp.wait_ge(delta_stored[i], NB * ET * 16)
                sp.wait_ge(du_stored[i], NB * ET * 16)
                sp.wait_ge(ud_stored[i], NB * LT * 8)
                sp.wait_ge(gz_stored[i], NB * LT * 16)
            sp.wait_ge(S["b_stored"], NB * 32)
            sp.wait_ge(S["ct_stored"], NB * 32)
            sp.wait_ge(S["ctx_loaded"], (NB + 1) * 16)
            sp.wait_ge(S["xa_loaded"], (NB + 1) * 16)
            sp.wait_ge(S["phase_a"], 4)

            def load_dd(c, par):
                sp.dma_start(dd[:, par], dd_d[bass.ds(c, 1)].rearrange("a p k t l -> p (a k) t l"))\
                    .then_inc(dd_loaded[par], 16)
                sp.dma_start(ct[:, par], ct_d[bass.ds(c, 1)].rearrange("a p c n -> p (a c) n"))\
                    .then_inc(dd_loaded[par], 16)

            def load_b(c, g):
                sp.dma_start(b_rows[:, g % 2],
                             b_d[bass.ds(c, 1), g * GR:(g + 1) * GR, :].partition_broadcast(P)
                             .rearrange("p a n t -> p (a n) t")).then_inc(b_loaded[g % 2], 16)

            def load_init(c):
                sp.dma_start(init[:], ud_d[bass.ds(c, 1)].rearrange("a c p e -> p (a c) e"))\
                    .then_inc(S["init_loaded"], 16)

            def load_end(c):
                sp.dma_start(gz[:], gz_d[bass.ds(c, 1)].rearrange("a c p e -> p (a c) e"))\
                    .then_inc(S["gz_loaded"], 16)
                sp.dma_start(x_in[:], x.rearrange("b (v c p) h -> (b v) p c h", p=P, c=CT)[bass.ds(c, 1)]
                             .rearrange("a p c h -> p (a c) h")).then_inc(S["x_loaded"], 16)

            load_dd(0, 0)
            load_b(0, 0)
            load_b(0, 1)
            load_init(0)
            load_end(0)

            def chunk(c, par, more=True, fin=2):
                if more:
                    after(sp, S["exp_done"], c * DS * ET)
                    settled(sp, S["passed_sp"])
                    after(sp, S["db_done"], c * DS)
                    settled(sp, S["passed_sp"])
                    after(sp, S["stt_done"], c * DS * CT)
                    settled(sp, S["passed_sp"])
                    load_dd(c + 1, 1 - par)
                for g in range(2, NG):
                    sp.wait_ge(S["db_done"], c * DS + (g - 1) * GR)
                    settled(sp, S["passed_sp"])
                    load_b(c, g)
                if more:
                    sp.wait_ge(S["stt_done"], c * DS * CT + CT)
                    settled(sp, S["passed_sp"])
                    load_init(c + 1)
                    for g in range(2):
                        sp.wait_ge(S["db_done"], c * DS + (g + NG - 1) * GR)
                        settled(sp, S["passed_sp"])
                        load_b(c + 1, g)

            def store(f):
                for tt in range(CT):
                    sp.wait_ge(S["out_ready"], f * CT + tt + 1)
                    settled(sp, S["passed_sp"])
                    sp.dma_start(out.rearrange("b (v c p) h -> (b v c) p h", p=P, c=CT)[bass.ds(f * CT + tt, 1)]
                                 .rearrange("a p h -> p (a h)"), out_sb[:, tt, :]).then_inc(out_stored[tt], 16)

            def next_end(c):
                sp.wait_ge(S["x1_ready"], (c + 1) * 2)
                settled(sp, S["passed_sp"])
                load_end(c + 1)

            chunk(0, 0)
            chunk(1, 1)
            next_end(0)
            with sp.Fori(1, NCH // 2 - 1) as p:
                for par in range(2):
                    c = p * 2 + par
                    chunk(c, par)
                    next_end(c - 1)
                    store(c - 2)
            chunk(NCH - 2, 0)
            next_end(NCH - 3)
            store(NCH - 4)
            chunk(NCH - 1, 1, more=False)
            next_end(NCH - 2)
            store(NCH - 3)
            store(NCH - 2)
            store(NCH - 1)
            for tt in range(CT):
                sp.wait_ge(out_stored[tt], NCH * 16)

        @block.gpsimd
        def _(pool):
            pool.memset(ident[:], 0.0).then_inc(S["ident_zero"], 1)
            pool.memset(half[:], -0.5).then_inc(S["half_ready"], 1)
            for i in range(2):
                pool.memset(xpad[:, i, 0:KC - 1], 0.0).then_inc(S["pad_zero"], 1)
            pool.wait_ge(S["ident_zero"], 1)
            pool.affine_select(out=ident[:], in_=ident[:], compare_op=ALU.not_equal, fill=1.0, base=0,
                               pattern=[[-1, P]], channel_multiplier=1).then_inc(S["ident_ready"], 1)
            pool.wait_ge(S["half_ready"], 1)
            pool.wait_ge(S["setup"], 1)

            def piece(b, s):
                pool.wait_ge(S["masks_ready"], b * PIECES + s + 1)
                after(pool, S["level"], b * PIECES + s)
                for j in range(ACT_AFF, NPAIR):
                    settled(pool, S["passed_pool"])
                    pool.tensor_scalar(pair[:, j, :], bit0[:, s % 2, :], lut_d[:, j:j + 1],
                                       lut_s[:, 2 * j:2 * j + 1], ALU.mult, ALU.add).then_inc(S["pairs_pool"], 1)

            def low_part(b, s):
                pool.wait_ge(S["whi_ready"], b * PIECES + s + 1)
                cols = bass.ds(b * (PIECES * PW) + s * PW, PW)
                pool.tensor_tensor(w_lo[:, cols], pair[:, 0, :], w_hi[:, cols], ALU.subtract)\
                    .then_inc(S["wlo_ready"], 1)

            def batch(b):
                pool.wait_ge(S["zstat"], b * 6 + 6)
                after(pool, S["zn_ready"], b * LT)
                pool.tensor_tensor(zsc[:, 2, :], zsc[:, 0, :], half[:], ALU.pow).then_inc(S["zpow"], 1)
                pool.wait_ge(S["zpow"], b * 2 + 1)
                settled(pool, S["passed_pool"])
                pool.tensor_scalar(zsc[:, 3, :], zsc[:, 2, :], 0.5, 1.0, ALU.mult, ALU.mult)\
                    .then_inc(S["zpow"], 1)
                pool.wait_ge(S["zpow"], b * 2 + 2)
                for st in range(LT):
                    if st == 0:
                        after(pool, S["gzt_ready"], b * LT)
                    settled(pool, S["passed_pool"])
                    pool.tensor_scalar(zn[:, st, :], x_sb[:, st, :], zsc[:, 1, st:st + 1], zsc[:, 3, st:st + 1],
                                       ALU.add, ALU.mult).then_inc(S["zn_ready"], 1)
                piece(b, 0)
                for s in range(1, 3):
                    low_part(b, s - 1)
                    piece(b, s)
                for et in range(ET):
                    pool.wait_ge(S["eexp_ready"], b * ET + et + 1)
                    settled(pool, S["passed_pool"])
                    pool.tensor_scalar(e_ln[:, et, :], e_exp[:, et, :], 1.0, 1.0, ALU.add, ALU.mult)\
                        .then_inc(S["w_ready"], 1)
                for s in range(3, 7):
                    low_part(b, s - 1)
                    piece(b, s)
                for et in range(ET):
                    pool.wait_ge(S["ln_ready"], b * ET + et + 1)
                    pool.wait_ge(S["t_ready"], b * ET + et + 1)
                    pool.tensor_tensor(e_ln[:, et, :], e_ln[:, et, :], e_exp[:, et, :], ALU.subtract)\
                        .then_inc(S["delta_ready"], 1)
                    pool.wait_ge(S["delta_ready"], b * (2 * ET) + 2 * et + 1)
                    after(pool, delta_stored[et % 2], b * 64 + 32 * (et // 2))
                    after(pool, du_stored[et % 2], b * 64 + 32 * (et // 2))
                    pool.tensor_tensor(delta_st[:, et % 2, :], e_ln[:, et, :], e_relu[:, et, :], ALU.add)\
                        .then_inc(S["delta_ready"], 1)
                    pool.wait_ge(S["delta_ready"], b * (2 * ET) + 2 * et + 2)
                    pool.tensor_tensor(du_st[:, et % 2, :], delta_st[:, et % 2, :], u_sb[:, et, :], ALU.mult)\
                        .then_inc(S["sp_ready"], 1)
                low_part(b, 6)
                piece(b, 7)
                low_part(b, 7)

            batch(0)
            with pool.Fori(1, NB) as b:
                batch(b)

            pool.wait_ge(S["wlo_ready"], NB * PIECES)
            pool.sem_inc(S["phase_a"], 1)
            pool.wait_ge(S["phase_a"], 4)

            def state(c, par, n):
                if n == 0:
                    pool.wait_ge(dd_loaded[par], c * 16 + (32 if par == 0 else 16))
                if n % GR == 0:
                    g = n // GR
                    pool.wait_ge(b_loaded[g % 2], c * (NG // 2 * 16) + 16 * (g // 2 + 1))
                after(pool, S["scan_done"], c * (DS * ET) + (n - 1) * ET)
                pool.tensor_tensor(
                    db[:, n % 2], dd[:, par, 1], b_rows[:, (n // GR) % 2, n % GR:n % GR + 1, :].to_broadcast([P, ET, TC]),
                    ALU.mult).then_inc(S["db_done"], 1)

            def normal(f):
                pool.wait_ge(S["fin_stat"], f * 4 + 4)
                after(pool, S["xn_ready"], f * CT)
                pool.tensor_tensor(nsc[:, 2, :], nsc[:, 0, :], half[:, 0:CT], ALU.pow).then_inc(S["npow"], 1)
                pool.wait_ge(S["npow"], f * 2 + 1)
                settled(pool, S["passed_pool"])
                pool.tensor_scalar(nsc[:, 3, :], nsc[:, 2, :], 256.0, 1.0, ALU.mult, ALU.mult)\
                    .then_inc(S["npow"], 1)
                pool.wait_ge(S["npow"], f * 2 + 2)
                after(pool, S["xnt_ready"], f * 2)

            def normal_rows(f, par):
                for tt in range(CT):
                    settled(pool, S["passed_pool"])
                    pool.tensor_scalar(xn[:, tt, :], x1[:, par, tt, :], nsc[:, 1, tt:tt + 1], nsc[:, 3, tt:tt + 1],
                                       ALU.add, ALU.mult).then_inc(S["xn_ready"], 1)

            def gated(f, g):
                two = 2 if g < JT // 2 else 1
                rp = rows(2 * g)
                slot = g % 2
                pool.wait_ge(S["q_ready"], f * JT + 2 * g + two)
                pool.wait_ge(S["us_ready"], f * JT + 2 * g + two)
                pool.tensor_tensor(u_gate[0:rp, slot, 0:two, :], q_gate[0:rp, slot, 0:two, :],
                                   u_gate[0:rp, slot, 0:two, :], ALU.mult).then_inc(S["hs_ready"], 1)

            def gated_low(f, g):
                two = 2 if g < JT // 2 else 1
                rp = rows(2 * g)
                slot = g % 2
                pool.wait_ge(S["hhi_ready"], f * 6 + g + 1)
                if g == 0:
                    after(pool, S["dn_ready"], f * CT)
                pool.tensor_tensor(h_lo[0:rp, 2 * g:2 * g + two, :], u_gate[0:rp, slot, 0:two, :],
                                   h_hi[0:rp, 2 * g:2 * g + two, :], ALU.subtract).then_inc(S["hlo_ready"], 1)

            def chunk(c, par, ssm, ffn):
                for n in range(DS):
                    if ssm:
                        state(c, par, n)
                    if ffn:
                        if n == 0:
                            normal(c - 1)
                            normal_rows(c - 1, 1 - par)
                        if n >= 6 and n % 2 == 0:
                            gated(c - 1, (n - 6) // 2)
                            if n >= 8:
                                gated_low(c - 1, (n - 8) // 2)
                        if n == DS - 1:
                            gated(c - 1, 5)
                            gated_low(c - 1, 4)
                            gated_low(c - 1, 5)

            chunk(0, 0, True, False)
            chunk(1, 1, True, True)
            with pool.Fori(1, NCH // 2) as p:
                for par in range(2):
                    chunk(p * 2 + par, par, True, True)
            chunk(NCH, 0, False, True)

        @block.scalar
        def _(act):
            act.wait_ge(S["vec_loaded"], 80)
            act.activation(neg_a[:], neg_a[:], ACT.Exp).then_inc(S["setup_act"], 1)
            act.mul(cb_half[:], vec[:, 0, :], 0.5).then_inc(S["setup_act"], 1)
            act.wait_ge(S["setup_act"], 2)
            act.mul(neg_a[:], neg_a[:], -1.0).then_inc(S["setup_act"], 1)
            act.wait_ge(S["pad_zero"], 2)
            act.wait_ge(S["setup"], 1)
            act.wait_ge(S["setup_act"], 3)

            def piece(b, s):
                act.wait_ge(S["masks_ready"], b * PIECES + s + 1)
                after(act, S["level"], b * PIECES + s)
                after(act, S["wlo_ready"], b * PIECES + s)
                for j in range(ACT_AFF):
                    act.activation(pair[:, j, :], bit0[:, s % 2, :], ACT.Identity, scale=lut_d[:, j:j + 1],
                                   bias=lut_s[:, 2 * j:2 * j + 1]).then_inc(S["pairs_act"], 1)

            def high_part(b, s):
                act.wait_ge(S["level"], b * PIECES + s + 1)
                act.copy(w_hi[:, bass.ds(b * (PIECES * PW) + s * PW, PW)], pair[:, 0, :])\
                    .then_inc(S["whi_ready"], 1)

            def pad(b, et):
                act.wait_ge(S["xp_ready"], b * ET + et + 1)
                after(act, S["v_ready"], b * ET + max(et - 1, 0))
                act.copy(xpad[:, et % 2, KC - 1:], bank[et % 2][:]).then_inc(S["xpad_ready"], 1)

            def gate_u(b, et):
                act.wait_ge(S["v_ready"], b * ET + et + 1)
                after(act, S["u_ready"], b * ET + max(et - 1, 0))
                act.activation(v_half[:, et % 2, :], bank[2 + et % 2][:], ACT.Identity, scale=0.5,
                               bias=cb_half[:, et:et + 1]).then_inc(S["vhalf_ready"], 1)
                act.activation(v_tanh[:, et % 2, :], bank[2 + et % 2][:], ACT.Tanh, scale=0.5,
                               bias=cb_half[:, et:et + 1]).then_inc(S["vhalf_ready"], 1)

            def batch(b):
                piece(b, 0)
                pad(b, 0)
                pad(b, 1)
                gate_u(b, 0)
                pad(b, 2)
                gate_u(b, 1)
                pad(b, 3)
                gate_u(b, 2)
                gate_u(b, 3)
                high_part(b, 0)
                piece(b, 1)
                for st in range(LT):
                    act.wait_ge(S["zn_ready"], b * LT + st + 1)
                    after(act, S["gz_ready"], b * LT + max(st - 1, 0))
                    act.activation(z_tanh[:, st % 2, :], zn[:, st, :], ACT.Tanh).then_inc(S["ztanh_ready"], 1)
                act.wait_ge(S["xdbl_ready"], b + 1)
                after(act, S["b_stored"], b * 32)
                after(act, S["ctt_ready"], b)
                act.copy(xdbl_sb[:], bank[4][0:NX, :]).then_inc(S["xdbl_sb_ready"], 1)
                high_part(b, 1)
                piece(b, 2)
                for et in range(ET):
                    act.wait_ge(S["dt_ready"], b * ET + et + 1)
                    if et == 0:
                        after(act, S["sp_ready"], b * ET)
                    after(act, S["eexp_ready"], b * ET + max(et - 1, 0))
                    act.activation(e_abs[:, et % 2, :], bank[et % 2][:], ACT.Abs, bias=vec[:, 1, et:et + 1])\
                        .then_inc(S["eabs_ready"], 1)
                    act.activation(e_relu[:, et, :], bank[et % 2][:], ACT.Relu, bias=vec[:, 1, et:et + 1])\
                        .then_inc(S["erelu_ready"], 1)
                    act.wait_ge(S["eabs_ready"], b * ET + et + 1)
                    act.activation(e_exp[:, et, :], e_abs[:, et % 2, :], ACT.Exp, scale=-1.0)\
                        .then_inc(S["eexp_ready"], 1)
                act.wait_ge(S["ctt_ready"], b + 1)
                after(act, S["ct_stored"], b * 32)
                act.copy(ct_st[:], bank[5][:, 0:LT * NX].rearrange("p (t k) -> p t k", k=NX)[:, :, DR + DS:NX])\
                    .then_inc(S["ct_ready"], 1)
                high_part(b, 2)
                piece(b, 3)
                for st in range(LT):
                    act.wait_ge(S["gzt_ready"], b * LT + st + 1)
                    after(act, gz_stored[st % 2], b * 64 + 32 * (st // 2))
                    act.copy(gz_st[:, st % 2], bank[7][:].rearrange("p (l s) -> p l s", s=P))\
                        .then_inc(S["gz_st_ready"], 1)
                high_part(b, 3)
                piece(b, 4)
                for tt in range(LT):
                    act.wait_ge(S["ud_ready"], b * LT + tt + 1)
                    after(act, ud_stored[tt % 2], b * 32 + 16 * (tt // 2))
                    act.copy(ud_st[:, tt % 2, :], bank[6][:]).then_inc(S["ud_free"], 1)
                high_part(b, 4)
                piece(b, 5)
                for et in range(ET):
                    act.wait_ge(S["t_ready"], b * ET + et + 1)
                    act.activation(e_ln[:, et, :], e_ln[:, et, :], ACT.Ln).then_inc(S["ln_ready"], 1)
                high_part(b, 5)
                piece(b, 6)
                high_part(b, 6)
                piece(b, 7)
                high_part(b, 7)

            batch(0)
            with act.Fori(1, NB) as b:
                batch(b)

            act.wait_ge(S["whi_ready"], NB * PIECES)
            act.sem_inc(S["phase_a"], 1)
            act.wait_ge(S["phase_a"], 4)

            def decay(c, par, n):
                if n == 0:
                    act.wait_ge(dd_loaded[par], c * 16 + (32 if par == 0 else 16))
                for et in range(ET):
                    if et % 2 == 0:
                        after(act, S["scan_done"], c * (DS * ET) + (n - 1) * ET + et + 2)
                    act.activation(bank[2 + et // 2][:, (et % 2) * TC:(et % 2 + 1) * TC], dd[:, par, 0, et, :],
                                   ACT.Exp, scale=neg_a[:, et, n:n + 1]).then_inc(S["exp_done"], 1)

            def high_x(f):
                for k in range(2):
                    act.wait_ge(S["xnt_ready"], f * 2 + k + 1)
                    if k == 0:
                        after(act, S["gu_ready"], f * JT)
                    act.copy(xt_hi[:, 2 * k:2 * k + 2, :], bank[4 + k][:].rearrange("p (a t) -> p a t", t=TC))\
                        .then_inc(S["xhi_ready"], 1)

            def gate(f, j):
                r = rows(j)
                act.wait_ge(S["gu_ready"], f * JT + j + 1)
                after(act, S["q_ready"], f * JT + j - 1)
                act.activation(g_tanh[0:r, j % 2, :], bank[4 + j % 2][0:r, 0:TC], ACT.Tanh,
                               scale=tanh_scale[0:r, :]).then_inc(S["gt_ready"], 1)
                if j % 2 == 0:
                    after(act, S["hlo_ready"], f * 6 + max(j // 2 - 1, 0))
                act.activation(u_gate[0:r, (j // 2) % 2, j % 2, :], bank[4 + j % 2][0:r, TC:2 * TC], ACT.Identity,
                               scale=2.0 ** -42).then_inc(S["us_ready"], 1)

            def high_h(f, g):
                two = 2 if g < JT // 2 else 1
                rp = rows(2 * g)
                act.wait_ge(S["hs_ready"], f * 6 + g + 1)
                if g == 0:
                    after(act, S["dn_ready"], f * CT)
                act.copy(h_hi[0:rp, 2 * g:2 * g + two, :], u_gate[0:rp, g % 2, 0:two, :])\
                    .then_inc(S["hhi_ready"], 1)

            def chunk(c, par, ssm, ffn):
                f = c - 1
                for n in range(DS):
                    if ssm:
                        decay(c, par, n)
                    if ffn:
                        if n == 1:
                            high_x(f)
                        if n > GU0 and n - GU0 - 1 < JT:
                            gate(f, n - GU0 - 1)
                        if n >= 7 and n % 2 == 1:
                            high_h(f, (n - 7) // 2)
                        if n == DS - 1:
                            high_h(f, 5)

            chunk(0, 0, True, False)
            chunk(1, 1, True, True)
            with act.Fori(1, NCH // 2) as p:
                for par in range(2):
                    chunk(p * 2 + par, par, True, True)
            chunk(NCH, 0, False, True)

        @block.vector
        def _(dve):
            step = S["picked"]
            dve.wait_ge(S["lut_loaded"], 16)
            dve.tensor_reduce(sc[:, 2:3], lut_in[:], AX.X, ALU.max, apply_absolute_value=True).then_inc(step, 1)
            dve.wait_ge(step, 1)
            dve.tensor_scalar(sc[:, 3:4], sc[:, 2:3], 1e-12, None, ALU.max).then_inc(step, 1)
            dve.wait_ge(step, 2)
            dve.tensor_scalar(lut_i[:, 0:1], sc[:, 3:4].bitcast(I32), 0x7F800000, None, ALU.bitwise_and)\
                .then_inc(step, 1)
            dve.wait_ge(step, 3)
            dve.tensor_scalar(lut_i[:, 1:2], lut_i[:, 0:1], -1.0, float(0x7F000000), ALU.mult, ALU.add)\
                .then_inc(step, 1)
            dve.wait_ge(step, 4)
            dve.tensor_scalar(lut_s[:], lut_in[:], lut_i[:, 1:2].bitcast(F32), 2.0 ** 10, ALU.mult, ALU.mult)\
                .then_inc(step, 1)
            dve.tensor_scalar(tanh_scale, lut_i[:, 0:1].bitcast(F32), 2.0 ** -19, None, ALU.mult)\
                .then_inc(step, 1)
            dve.tensor_scalar(sc[:, 4:5], lut_i[:, 0:1].bitcast(F32), lut_i[:, 0:1].bitcast(F32), None, ALU.mult)\
                .then_inc(step, 1)
            dve.wait_ge(step, 7)
            dve.tensor_scalar(out_scale, sc[:, 4:5], lut_i[:, 0:1].bitcast(F32), 2.0 ** -5, ALU.mult, ALU.mult)\
                .then_inc(step, 1)
            pairs = lut_s[:].rearrange("p (j two) -> p j two", two=2)
            dve.tensor_tensor(lut_d[:], pairs[:, :, 1], pairs[:, :, 0], ALU.subtract).then_inc(step, 1)
            dve.wait_ge(step, 9)
            dve.sem_inc(S["setup"], 1)
            dve.wait_ge(S["vec_loaded"], 80)
            dve.wait_ge(S["ident_ready"], 1)
            for et in range(ET):
                for k in range(KC):
                    dve.tensor_scalar(conv_diag[:, et, k, :], ident[:], cw_sb[:, et, k:k + 1], None, ALU.mult)\
                        .then_inc(S["setup"], 1)
                dve.tensor_scalar(d_diag[:, et, :], ident[:], vec[:, 2, et:et + 1], None, ALU.mult)\
                    .then_inc(S["setup"], 1)

            def batch(b):
                def piece_masks(s):
                    dve.wait_ge(idx_loaded[s % 2], b * (PIECES * 8) + 16 * (s // 2) + 16)
                    after(dve, S["pairs_act"], b * (PIECES * ACT_AFF) + max(s - 1, 0) * ACT_AFF)
                    after(dve, S["pairs_pool"], b * (PIECES * (NPAIR - ACT_AFF)) + max(s - 1, 0) * (NPAIR - ACT_AFF))
                    after(dve, S["level"], b * PIECES + s)
                    dve.tensor_scalar(bit0[:, s % 2, :], idx_sb[:, s % 2, :], 1, None, ALU.bitwise_and)
                    for i in range(3):
                        m = dve.tensor_scalar(bits[:, i, :], idx_sb[:, s % 2, :], 2 << i, None, ALU.bitwise_and)
                    m.then_inc(S["masks_ready"], 1)

                def piece_select(s):
                    dve.wait_ge(S["masks_ready"], b * PIECES + s + 1)
                    dve.wait_ge(S["pairs_act"], b * (PIECES * ACT_AFF) + (s + 1) * ACT_AFF)
                    dve.wait_ge(S["pairs_pool"], b * (PIECES * (NPAIR - ACT_AFF)) + (s + 1) * (NPAIR - ACT_AFF))
                    for i, inc in ((0, S["picked"]), (1, S["picked"]), (2, S["level"])):
                        k = NPAIR >> (i + 1)
                        dst = pair[:].rearrange("p (k two r) w -> p k two r w", two=2, r=1 << i)
                        if i:
                            dve.wait_ge(S["picked"], b * (2 * PIECES) + (9 + 2 * s + i))
                        settled(dve, S["passed_dve"])
                        dve.copy_predicated(dst[:, :, 0, 0, :], bits[:, i:i + 1, :].to_broadcast([P, k, PW]),
                                            dst[:, :, 1, 0, :]).then_inc(inc, 1)

                piece_masks(0)
                dve.wait_ge(S["xa_loaded"], b * 16 + 16)
                for st in range(LT):
                    dve.bn_stats(stats[:, st, :], x_sb[:, st, :]).then_inc(S["zstat"], 1)
                dve.wait_ge(S["zstat"], b * 6 + 4)
                settled(dve, S["passed_dve"])
                for st in range(LT):
                    m = dve.bn_aggr(mv[:, st, :], stats[:, st, :])
                m.then_inc(S["zsc_ready"], 1)
                dve.wait_ge(S["zsc_ready"], b + 1)
                after(dve, S["zn_ready"], b * LT)
                dve.tensor_scalar(zsc[:, 0, :], mv[:, :, 1], EPS, None, ALU.add).then_inc(S["zstat"], 1)
                dve.tensor_scalar(zsc[:, 1, :], mv[:, :, 0], -1.0, None, ALU.mult).then_inc(S["zstat"], 1)
                for et in range(ET):
                    dve.wait_ge(S["vhalf_ready"], b * (2 * ET) + 2 * et + 2)
                    if et == 0:
                        after(dve, S["sp_ready"], b * ET)
                        after(dve, S["ud_ready"], b * LT)
                    dve.scalar_tensor_tensor(u_sb[:, et, :], v_tanh[:, et % 2, :], 1.0, v_half[:, et % 2, :],
                                             ALU.add, ALU.mult).then_inc(S["u_ready"], 1)
                piece_select(0)
                piece_masks(1)
                for st in range(LT):
                    dve.wait_ge(S["ztanh_ready"], b * LT + st + 1)
                    dve.scalar_tensor_tensor(zn[:, st, :], z_tanh[:, st % 2, :], 1.0, zn[:, st, :],
                                             ALU.add, ALU.mult).then_inc(S["gz_ready"], 1)
                piece_select(1)
                piece_masks(2)
                piece_select(2)
                piece_masks(3)
                for et in range(ET):
                    dve.wait_ge(S["w_ready"], b * ET + et + 1)
                    dve.scalar_tensor_tensor(e_exp[:, et, :], e_ln[:, et, :], 1.0, e_exp[:, et, :],
                                             ALU.subtract, ALU.subtract).then_inc(S["t_ready"], 1)
                for s in range(3, PIECES):
                    piece_select(s)
                    if s + 1 < PIECES:
                        piece_masks(s + 1)

            batch(0)
            with dve.Fori(1, NB) as b:
                batch(b)

            dve.wait_ge(S["level"], NB * PIECES)
            dve.wait_ge(S["setup"], 1 + ET * (KC + 1))
            dve.sem_inc(S["phase_a"], 1)
            dve.wait_ge(S["phase_a"], 4)

            def scans(c, par, n):
                dve.wait_ge(S["db_done"], c * DS + n + 1)
                after(dve, S["ht_ready"], c * (DS * CT) + (n - 1) * CT)
                if par == 0:
                    after(dve, S["hl_saved"], (c * (DS // 2) + n - 1) if n else c * (DS // 2))
                elif n < 2:
                    dve.wait_ge(S["hl_saved"], c * (DS // 2) + (DS // 2 - 1) + n)
                for et in range(ET):
                    if et % 2 == 0:
                        dve.wait_ge(S["exp_done"], c * (DS * ET) + n * ET + et + 2)
                    first = 0.0 if par == 0 else h_last[:, n, et:et + 1]
                    dve.tensor_tensor_scan(h[:, n % 2, et, :],
                                           bank[2 + et // 2][:, (et % 2) * TC:(et % 2 + 1) * TC],
                                           db[:, n % 2, et, :], first, ALU.mult, ALU.add)\
                        .then_inc(S["scan_done"], 1)

            def outputs(c, par, n):
                for tt in range(CT):
                    dve.wait_ge(S["ht_ready"], c * (DS * CT) + n * CT + tt + 1)
                    if n == 0:
                        if tt == 0:
                            dve.wait_ge(S["init_loaded"], c * 16 + 16)
                            after(dve, S["x1_ready"], c * 2)
                        base = init
                    else:
                        dve.wait_ge(S["stt_done"], c * (DS * CT) + (n - 1) * CT + tt + 1)
                        base = acc
                    dve.scalar_tensor_tensor(acc[:, tt, :], bank[tt][:], ct[:, par, tt, n:n + 1], base[:, tt, :],
                                             ALU.mult, ALU.add).then_inc(S["stt_done"], 1)
                if par == 0:
                    dve.wait_ge(S["scan_done"], c * (DS * ET) + (n + 1) * ET)
                    dve.tensor_copy(h_last[:, n, :], h[:, n % 2, :, TC - 1]).then_inc(S["hl_saved"], 1)

            def finish(c, par):
                dve.wait_ge(S["stt_done"], (c + 1) * (DS * CT))
                dve.wait_ge(S["gz_loaded"], c * 16 + 16)
                dve.tensor_tensor(x1[:, par], acc[:], gz[:], ALU.mult).then_inc(S["x1_ready"], 1)
                dve.wait_ge(S["x_loaded"], c * 16 + 16)
                dve.wait_ge(S["x1_ready"], c * 2 + 1)
                dve.tensor_tensor(x1[:, par], x1[:, par], x_in[:], ALU.add).then_inc(S["x1_ready"], 1)
                dve.wait_ge(S["x1_ready"], c * 2 + 2)
                for tt in range(CT):
                    m = dve.bn_stats(stats2[:, tt, :], x1[:, par, tt, :])
                m.then_inc(S["fin_stat"], 1)
                dve.wait_ge(S["fin_stat"], c * 4 + 1)
                settled(dve, S["passed_dve"])
                for tt in range(CT):
                    m = dve.bn_aggr(mv2[:, tt, :], stats2[:, tt, :])
                m.then_inc(S["fin_stat"], 1)
                dve.wait_ge(S["fin_stat"], c * 4 + 2)
                after(dve, S["xn_ready"], c * CT)
                dve.tensor_scalar(nsc[:, 0, :], mv2[:, :, 1], EPS, None, ALU.add).then_inc(S["fin_stat"], 1)
                dve.tensor_scalar(nsc[:, 1, :], mv2[:, :, 0], -1.0, None, ALU.mult).then_inc(S["fin_stat"], 1)

            def low_x(f):
                for k in range(2):
                    dve.wait_ge(S["xhi_ready"], f * 2 + k + 1)
                    if k == 0:
                        after(dve, S["gu_ready"], f * JT)
                    dve.tensor_tensor(xt_lo[:, 2 * k:2 * k + 2, :], bank[4 + k][:].rearrange("p (a t) -> p a t", t=TC),
                                      xt_hi[:, 2 * k:2 * k + 2, :], ALU.subtract).then_inc(S["xlo_ready"], 1)

            def gate(f, j):
                r = rows(j)
                dve.wait_ge(S["us_ready"], f * JT + j + 1)
                if j % 2 == 0:
                    after(dve, S["hs_ready"], f * 6 + max(j // 2 - 1, 0))
                dve.scalar_tensor_tensor(q_gate[0:r, (j // 2) % 2, j % 2, :], g_tanh[0:r, j % 2, :], 1.0,
                                         bank[4 + j % 2][0:r, 0:TC], ALU.add, ALU.mult).then_inc(S["q_ready"], 1)

            def result(f, par, tt):
                dve.wait_ge(S["dn_ready"], f * CT + tt + 1)
                after(dve, out_stored[tt], f * 16)
                dve.scalar_tensor_tensor(out_sb[:, tt, :], bank[6 + tt][:], out_scale, x1[:, par, tt, :],
                                         ALU.mult, ALU.add).then_inc(S["out_ready"], 1)

            def chunk(c, par, ssm, ffn, down):
                f = c - 1
                for n in range(DS):
                    if ssm:
                        scans(c, par, n)
                        if n:
                            outputs(c, par, n - 1)
                    if n == 0 and ffn:
                        outputs(f, 1 - par, DS - 1)
                        finish(f, 1 - par)
                    if down and n in (1, 2):
                        result(c - 2, par, n - 1)
                    if ffn:
                        if n == 1:
                            low_x(f)
                        if n > GU0 and n - GU0 - 1 < JT:
                            gate(f, n - GU0 - 1)

            chunk(0, 0, True, False, False)
            chunk(1, 1, True, True, False)
            with dve.Fori(1, NCH // 2) as p:
                for par in range(2):
                    chunk(p * 2 + par, par, True, True, True)
            chunk(NCH, 0, False, True, True)
            for tt in range(CT):
                result(NCH - 1, 1, tt)

        @block.tensor
        def _(pe):
            pe.wait_ge(S["params_loaded"], 48)
            pe.wait_ge(S["ident_ready"], 1)
            pe.wait_ge(S["setup"], 1 + ET * (KC + 1))

            def in_proj(b, et):
                after(pe, S["xpad_ready"], b * ET + max(et - 1, 0))
                if et < 2:
                    after(pe, S["eexp_ready"], b * ET)
                    after(pe, S["erelu_ready"], b * ET)
                for k in range(KM):
                    m = pe.matmul(bank[et % 2][:], win_sb[:, k, et * P:(et + 1) * P], ctx_sb[:, k, :],
                                  start=(k == 0), stop=(k == KM - 1))
                m.then_inc(S["xp_ready"], 1)

            def conv(b, et):
                pe.wait_ge(S["xpad_ready"], b * ET + et + 1)
                after(pe, S["vhalf_ready"], b * (2 * ET) + 2 * max(et - 1, 0))
                for k in range(KC):
                    m = pe.matmul(bank[2 + et % 2][:], conv_diag[:, et, k, :], xpad[:, et % 2, k:k + L],
                                  start=(k == 0), stop=(k == KC - 1))
                m.then_inc(S["v_ready"], 1)

            def batch(b):
                pe.wait_ge(S["ctx_loaded"], b * 16 + 16)
                in_proj(b, 0)
                in_proj(b, 1)
                conv(b, 0)
                in_proj(b, 2)
                conv(b, 1)
                in_proj(b, 3)
                conv(b, 2)
                conv(b, 3)
                after(pe, S["xdbl_sb_ready"], b)
                for et in range(ET):
                    pe.wait_ge(S["u_ready"], b * ET + et + 1)
                    m = pe.matmul(bank[4][0:NX, :], xproj_sb[:, et, :], u_sb[:, et, :],
                                  start=(et == 0), stop=(et == ET - 1))
                m.then_inc(S["xdbl_ready"], 1)
                pe.wait_ge(S["xdbl_sb_ready"], b + 1)
                for et in range(ET):
                    if et >= 2:
                        pe.wait_ge(S["eexp_ready"], b * ET + et - 1)
                        pe.wait_ge(S["erelu_ready"], b * ET + et - 1)
                    else:
                        pe.wait_ge(S["xpad_ready"], b * ET + ET)
                    pe.matmul(bank[et % 2][:], dt_sb[:, et * P:(et + 1) * P], xdbl_sb[0:DR, :],
                              start=True, stop=True).then_inc(S["dt_ready"], 1)
                after(pe, S["ct_ready"], b)
                settled(pe, S["passed_pe"])
                for tt in range(LT):
                    m = pe.transpose(bank[5][:, tt * NX:(tt + 1) * NX], xdbl_sb[:, tt * P:(tt + 1) * P],
                                     ident[0:NX, 0:NX])
                m.then_inc(S["ctt_ready"], 1)
                for st in range(LT):
                    pe.wait_ge(S["gz_ready"], b * LT + st + 1)
                    after(pe, S["gz_st_ready"], b * LT + st)
                    for lt in range(LT):
                        m = pe.transpose(bank[7][:, lt * P:(lt + 1) * P], zn[:, st, lt * P:(lt + 1) * P], ident[:])
                    m.then_inc(S["gzt_ready"], 1)
                for tt in range(LT):
                    after(pe, S["ud_free"], b * LT + tt)
                    for et in range(ET):
                        m = pe.matmul(bank[6][:, et * P:(et + 1) * P], u_sb[:, et, tt * P:(tt + 1) * P],
                                      d_diag[:, et, :], start=True, stop=True)
                    m.then_inc(S["ud_ready"], 1)

            batch(0)
            with pe.Fori(1, NB) as b:
                batch(b)

            pe.wait_ge(S["ud_free"], NB * LT)
            pe.wait_ge(S["gz_st_ready"], NB * LT)
            pe.wait_ge(S["ct_ready"], NB)
            pe.wait_ge(S["eexp_ready"], NB * ET)
            pe.wait_ge(S["gzt_ready"], NB * LT)
            pe.sem_inc(S["phase_a"], 1)
            pe.wait_ge(S["phase_a"], 4)

            def turn(c, n):
                for tt in range(CT):
                    after(pe, S["stt_done"], c * (DS * CT) + (n - 1) * CT + tt + 1)
                    for et in range(ET):
                        if tt == 0:
                            pe.wait_ge(S["scan_done"], c * (DS * ET) + n * ET + et + 1)
                        m = pe.transpose(bank[tt][:, et * P:(et + 1) * P], h[:, n % 2, et, tt * P:(tt + 1) * P],
                                         ident[:])
                    m.then_inc(S["ht_ready"], 1)

            def turn_x(f):
                for k in range(2):
                    after(pe, S["q_ready"], f * JT)
                    after(pe, S["us_ready"], f * JT)
                    pe.wait_ge(S["xn_ready"], f * CT + CT)
                    for a in range(2):
                        for tt in range(CT):
                            kt = 2 * k + a
                            m = pe.transpose(bank[4 + k][:, a * TC + tt * P:a * TC + (tt + 1) * P],
                                             xn[:, tt, kt * P:(kt + 1) * P], ident[:])
                    m.then_inc(S["xnt_ready"], 1)

            def gate_up(f, j):
                r = rows(j)
                if j == 0:
                    pe.wait_ge(S["xlo_ready"], f * 2 + 2)
                else:
                    after(pe, S["q_ready"], f * JT + j - 1)
                    after(pe, S["us_ready"], f * JT + j - 1)
                for part, w0 in ((0, 0), (TC, UP0)):
                    i = 0
                    for kt in range(KT):
                        cols = slice(w0 + kt * INTER + j * P, w0 + kt * INTER + j * P + r)
                        for w, v in ((w_hi, xt_hi), (w_hi, xt_lo), (w_lo, xt_hi)):
                            m = pe.matmul(bank[4 + j % 2][0:r, part:part + TC], w[:, cols], v[:, kt, :],
                                          start=(i == 0), stop=(i == 3 * KT - 1))
                            i += 1
                m.then_inc(S["gu_ready"], 1)

            def down(f, part):
                for tt, j in down_parts[part]:
                    r = rows(j)
                    if j % 2 == 0 and tt == 0:
                        pe.wait_ge(S["hlo_ready"], f * 6 + j // 2 + 1)
                    if j == 0:
                        after(pe, S["out_ready"], f * CT - CT + tt + 1)
                    cols = slice(DN0 + j * HID, DN0 + (j + 1) * HID)
                    toks = slice(tt * P, (tt + 1) * P)
                    for i, (v, w) in enumerate(((h_hi, w_hi), (h_hi, w_lo), (h_lo, w_hi))):
                        m = pe.matmul(bank[6 + tt][:], v[0:r, j, toks], w[0:r, cols],
                                      start=(j == 0 and i == 0), stop=(j == JT - 1 and i == 2))
                    if j == JT - 1:
                        m.then_inc(S["dn_ready"], 1)

            def chunk(c, ssm, ffn, rest):
                f = c - 1
                for n in range(DS):
                    if rest and n < 2:
                        down(c - 2, 2 + n)
                    if ssm:
                        turn(c, n)
                    if ffn:
                        if n == 1:
                            turn_x(f)
                        if n >= GU0 and n - GU0 < JT:
                            gate_up(f, n - GU0)
                        if n >= DS - 2:
                            down(f, n - DS + 2)

            chunk(0, True, False, False)
            chunk(1, True, True, False)
            with pe.Fori(1, NCH // 2) as p:
                for par in range(2):
                    chunk(p * 2 + par, True, True, True)
            chunk(NCH, False, True, True)
            down(NCH - 1, 2)
            down(NCH - 1, 3)


def kernel(x, ctx_1024, L0_xattn_in_proj_w, L0_xattn_conv_w, L0_xattn_conv_b, L0_xattn_x_proj_w,
           L0_xattn_dt_proj_w, L0_xattn_dt_proj_b, L0_xattn_A_log, L0_xattn_D, L0_ffn_lut,
           L0_ffn_gate_idx, L0_ffn_up_idx, L0_ffn_down_idx):
    import numpy as np
    import concourse.bacc as bacc
    from concourse.bass_utils import run_bass_kernel_spmd

    part = 128

    def tiles(a):
        a = np.asarray(a)
        n = -(-a.shape[0] // part)
        full = np.zeros((n * part, a.shape[1]), a.dtype)
        full[:a.shape[0]] = a
        return full.reshape(n, part, a.shape[1]).transpose(1, 0, 2).reshape(part, -1)

    def lay(a):
        return np.ascontiguousarray(np.asarray(a))

    arrays = {
        "ctx_t": lay(np.asarray(ctx_1024).transpose(0, 2, 1)),
        "x": lay(x),
        "win_t": lay(np.asarray(L0_xattn_in_proj_w).T),
        "conv_w": lay(L0_xattn_conv_w),
        "conv_b": lay(L0_xattn_conv_b),
        "xproj_t": lay(np.asarray(L0_xattn_x_proj_w).T),
        "dt_t": lay(np.asarray(L0_xattn_dt_proj_w).T),
        "dt_b": lay(L0_xattn_dt_proj_b),
        "a_log": lay(L0_xattn_A_log),
        "d_skip": lay(L0_xattn_D),
        "lut": lay(L0_ffn_lut),
        "idx": lay(np.concatenate([tiles(np.asarray(L0_ffn_gate_idx).T), tiles(np.asarray(L0_ffn_up_idx).T),
                                   tiles(np.asarray(L0_ffn_down_idx).T)], axis=1)),
    }
    nc = bacc.Bacc("TRN2", target_bir_lowering=False, num_devices=1)
    args = [nc.dram_tensor(f"in_{k}", a.shape, mybir.dt.from_np(a.dtype), kind="ExternalInput").ap()
            for k, a in arrays.items()]
    out = nc.dram_tensor("out_0", arrays["x"].shape, F32, kind="ExternalOutput").ap()
    mamba_ffn(nc, *args, out)
    r = run_bass_kernel_spmd(nc, [{f"in_{k}": a for k, a in arrays.items()}], core_ids=[0])
    return r.results[0]["out_0"]
```

```python
from contextlib import ExitStack

import concourse.bass as bass
import concourse.mybir as mybir

ALU = mybir.AluOpType
ACT = mybir.ActivationFunctionType
AX = mybir.AxisListType
F32 = mybir.dt.float32
F16 = mybir.dt.float16
I32 = mybir.dt.int32

P = 128
EPS = 1e-5


def after(eng, sem, count):
    if isinstance(count, int) and count <= 0:
        return
    eng.wait_ge(sem, count)


def settled(eng, sem):
    eng.sem_inc(sem, 1)


def mamba_ffn(nc, ctx_t, x, win_t, conv_w, conv_b, xproj_t, dt_t, dt_b, a_log, d_skip, lut, idx, out):
    NB, DM, L = ctx_t.shape
    DI = win_t.shape[1]
    DS = a_log.shape[1]
    DR = dt_t.shape[0]
    KC = conv_w.shape[1]
    NX = xproj_t.shape[1]
    NLUT = lut.shape[0]
    HID = x.shape[2]
    F = idx.shape[1]
    INTER = 1376
    KT = HID // P
    ET = DI // P
    KM = DM // P
    LT = L // P
    JT = -(-INTER // P)
    TC = 256
    CT = TC // P
    NCH = NB * L // TC
    UP0 = KT * INTER
    DN0 = 2 * KT * INTER
    PIECES = 8
    PW = F // (NB * PIECES)
    ACT_AFF = 4
    NPAIR = NLUT // 2
    GR = 4
    NG = DS // GR
    assert F == NB * PIECES * PW and F == DN0 + JT * HID and L == CT * P * 2
    assert NX == DR + 2 * DS

    def rows(j):
        return min(P, INTER - j * P)

    def dram(name, shape):
        return nc.dram_tensor(name, shape, F32, kind="Internal").ap()

    dd_d = dram("dd_scratch", [NCH, P, 2, ET, TC])
    b_d = dram("b_scratch", [NCH, DS, TC])
    ct_d = dram("ct_scratch", [NCH, P, CT, DS])
    ud_d = dram("ud_scratch", [NCH, CT, P, DI])
    gz_d = dram("gz_scratch", [NCH, CT, P, L])

    ctx = ExitStack()
    with ctx:
        def sem(name):
            return ctx.enter_context(nc.semaphore(name))

        def sb(name, shape, dt=F32):
            return ctx.enter_context(nc.sbuf_tensor(name, shape, dt))

        bank = [ctx.enter_context(nc.psum_tensor(f"bank{i}", [P, 512], F32)) for i in range(8)]

        w_hi = sb("w_hi", [P, F], F16)
        w_lo = sb("w_lo", [P, F], F16)
        ident = sb("ident", [P, P])
        neg_a = sb("neg_a", [P, ET, DS])
        sc = sb("sc", [P, 8])
        lut_s = sb("lut_s", [P, NLUT])
        lut_d = sb("lut_d", [P, NPAIR])
        half = sb("half", [P, LT])
        out_scale, tanh_scale = sc[:, 0:1], sc[:, 1:2]

        ctxA = ExitStack()

        def sa(name, shape, dt=F32):
            return ctxA.enter_context(nc.sbuf_tensor(name, shape, dt))

        ctx_sb = sa("ctx_sb", [P, KM, L])
        x_sb = sa("x_sb", [P, LT, HID])
        win_sb = sa("win_sb", [P, KM, DI])
        xproj_sb = sa("xproj_sb", [P, ET, NX])
        dt_sb = sa("dt_sb", [DR, DI])
        xdbl_sb = sa("xdbl_sb", [NX, L])
        conv_diag = sa("conv_diag", [P, ET, KC, P])
        d_diag = sa("d_diag", [P, ET, P])
        cw_sb = sa("cw_sb", [P, ET, KC])
        vec = sa("vec", [P, 3, ET])
        cb_half = sa("cb_half", [P, ET])
        xpad = sa("xpad", [P, 2, L + KC - 1])
        v_half = sa("v_half", [P, 2, L])
        v_tanh = sa("v_tanh", [P, 2, L])
        u_sb = sa("u_sb", [P, ET, L])
        e_exp = sa("e_exp", [P, ET, L])
        e_ln = sa("e_ln", [P, ET, L])
        e_relu = sa("e_relu", [P, ET, L])
        ud_st = sa("ud_st", [P, 2, DI])
        gz_st = sa("gz_st", [P, 2, LT, P])
        ct_st = sa("ct_st", [P, LT, DS])
        zn = sa("zn", [P, LT, HID])
        stats = sa("stats", [P, LT, 6])
        mv = sa("mv", [P, LT, 2])
        zsc = sa("zsc", [P, 4, LT])
        idx_sb = sa("idx_sb", [P, 2, PW], I32)
        bit0 = sa("bit0", [P, 2, PW], I32)
        bits = sa("bits", [P, 3, PW], I32)
        pair = sa("pair", [P, 2, NPAIR, PW])
        lut_in = sa("lut_in", [P, NLUT])
        lut_i = sa("lut_i", [P, 4], I32)
        ctxA.close()

        ctxB = ctx.enter_context(ExitStack())

        def sB(name, shape, dt=F32):
            return ctxB.enter_context(nc.sbuf_tensor(name, shape, dt))

        dd = sB("dd", [P, 2, 2, ET, TC])
        b_rows = sB("b_rows", [P, 2, GR, TC])
        ct = sB("ct", [P, 2, CT, DS])
        db = sB("db", [P, 2, ET, TC])
        h = sB("h", [P, 2, ET, TC])
        h_last = sB("h_last", [P, DS, ET])
        init = sB("init", [P, CT, DI])
        acc = sB("acc", [P, CT, DI])
        gz = sB("gz", [P, CT, DI])
        x_in = sB("x_in", [P, CT, HID])
        x1 = sB("x1", [P, 2, CT, HID])
        xn = sB("xn", [P, CT, HID])
        xt_hi = sB("xt_hi", [P, KT, TC], F16)
        xt_lo = sB("xt_lo", [P, KT, TC], F16)
        g_tanh = sB("g_tanh", [P, 2, TC])
        u_gate = sB("u_gate", [P, 2, 2, TC])
        q_gate = sB("q_gate", [P, 2, 2, TC])
        h_hi = sB("h_hi", [P, JT + 1, TC], F16)
        h_lo = sB("h_lo", [P, JT + 1, TC], F16)
        out_sb = sB("out_sb", [P, CT, HID])
        stats2 = sB("stats2", [P, CT, 6])
        mv2 = sB("mv2", [P, CT, 2])
        nsc = sB("nsc", [P, 4, CT])

        names = """params_loaded lut_loaded vec_loaded ctx_loaded xa_loaded ident_zero ident_ready setup setup_act
            half_ready xp_ready xpad_ready pad_zero v_ready vhalf_ready u_ready xdbl_ready xdbl_sb_ready ud_ready
            ud_free dt_ready eabs_ready erelu_ready eexp_ready w_ready t_ready ln_ready sp_ready delta_ready
            ctt_ready ct_ready zstat zsc_ready zpow zn_ready ztanh_ready gz_ready gzt_ready gz_st_ready
            bit0_ready masks_ready pairs_act pairs_pool level picked whi_ready wlo_ready
            b_stored ct_stored dd_stored phase_a scan_done exp_done db_done ht_ready stt_done hl_saved b_used
            init_loaded gz_loaded x_loaded x1_ready fin_stat nsc_ready npow xn_ready xnt_ready xhi_ready xlo_ready
            gu_ready gt_ready us_ready q_ready hs_ready hhi_ready hlo_ready dn_ready out_ready
            passed_sp passed_pool passed_dve passed_pe""".split()
        S = {name: sem(name) for name in names}
        idx_loaded = [sem(f"idx_loaded{i}") for i in range(2)]
        ud_stored = [sem(f"ud_stored{i}") for i in range(2)]
        gz_stored = [sem(f"gz_stored{i}") for i in range(2)]
        dd_loaded = [sem(f"dd_loaded{i}") for i in range(2)]
        b_loaded = [sem(f"b_loaded{i}") for i in range(2)]
        out_stored = [sem(f"out_stored{i}") for i in range(CT)]

        block = ctx.enter_context(nc.Block())

        down_parts = [
            [(0, j) for j in range(5)],
            [(0, j) for j in range(5, 8)] + [(1, j) for j in range(3)],
            [(0, j) for j in range(8, JT)] + [(1, j) for j in range(3, 6)],
            [(1, j) for j in range(6, JT)],
        ]
        GU0 = 3

        @block.sync
        def _(sp):
            sp.dma_start(lut_in[:], lut.rearrange("(a n) -> a n", a=1).partition_broadcast(P)
                         .rearrange("p a n -> p (a n)")).then_inc(S["lut_loaded"], 16)
            sp.dma_start(win_sb[:], win_t.rearrange("(k p) e -> p k e", p=P)).then_inc(S["params_loaded"], 16)
            sp.dma_start(cw_sb[:], conv_w.rearrange("(t p) k -> p t k", p=P)).then_inc(S["vec_loaded"], 16)
            with nc.allow_non_contiguous_dma(reason="512 numbers each"):
                for i, v in enumerate((conv_b, dt_b, d_skip)):
                    sp.dma_start(vec[:, i, :], v.rearrange("(t p) -> p t", p=P)).then_inc(S["vec_loaded"], 16)
            sp.dma_start(neg_a[:], a_log.rearrange("(t p) n -> p t n", p=P)).then_inc(S["vec_loaded"], 16)
            sp.dma_start(xproj_sb[:], xproj_t.rearrange("(t p) k -> p t k", p=P)).then_inc(S["params_loaded"], 16)
            sp.dma_start(dt_sb[:], dt_t).then_inc(S["params_loaded"], 16)

            def load_ctx(b):
                sp.dma_start(ctx_sb[:], ctx_t[bass.ds(b, 1)].rearrange("a (k p) l -> p (a k) l", p=P))\
                    .then_inc(S["ctx_loaded"], 16)

            def load_x(b):
                sp.dma_start(x_sb[:], x[bass.ds(b, 1)].rearrange("a (s p) h -> p (a s) h", p=P))\
                    .then_inc(S["xa_loaded"], 16)

            def load_idx(b, s):
                sp.dma_start(idx_sb[:, s % 2, :], idx[:, bass.ds(b * (PIECES * PW) + s * PW, PW)])\
                    .then_inc(idx_loaded[s % 2], 16)

            def half_view(d, b, hf):
                return d[bass.ds(b * 2 + hf, 1)]

            def store_ud(b, tts):
                for tt in tts:
                    sp.wait_ge(S["ud_free"], b * LT + tt + 1)
                    settled(sp, S["passed_sp"])
                    sp.dma_start(half_view(ud_d, b, tt // CT)[:, tt % CT].rearrange("a p e -> p (a e)"),
                                 ud_st[:, tt % 2, :]).then_inc(ud_stored[tt % 2], 16)

            def store_gz(b, sts):
                for st in sts:
                    sp.wait_ge(S["gz_st_ready"], b * LT + st + 1)
                    settled(sp, S["passed_sp"])
                    for hf in range(2):
                        sp.dma_start(
                            half_view(gz_d, b, hf)[:, :, :, st * P:(st + 1) * P].rearrange("a c p s -> p (a c) s"),
                            gz_st[:, st % 2, hf * CT:(hf + 1) * CT, :]).then_inc(gz_stored[st % 2], 16)

            def store_dd(b, et):
                sp.wait_ge(S["sp_ready"], b * ET + et + 1)
                settled(sp, S["passed_sp"])
                dst = dd_d[bass.ds(b * 2, 2)]
                for i, src in enumerate((e_relu, e_ln)):
                    sp.dma_start(dst[:, :, i, et, :].rearrange("c p t -> p c t"),
                                 src[:, et, :].rearrange("p (c t) -> p c t", t=TC)).then_inc(S["dd_stored"], 16)

            load_idx(0, 0)
            load_ctx(0)
            load_x(0)
            load_idx(0, 1)

            def batch(b, last=False):
                for s in range(PIECES):
                    if not (last and s + 2 >= PIECES):
                        sp.wait_ge(S["masks_ready"], b * PIECES + s + 1)
                        settled(sp, S["passed_sp"])
                        load_idx(b, s + 2)
                    if s == 0 and not last:
                        sp.wait_ge(S["xp_ready"], b * ET + ET)
                        settled(sp, S["passed_sp"])
                        load_ctx(b + 1)
                    if s == 1:
                        sp.wait_ge(S["xdbl_sb_ready"], b + 1)
                        settled(sp, S["passed_sp"])
                        sp.dma_start(b_d[bass.ds(b * 2, 2)].rearrange("c n t -> n c t"),
                                     xdbl_sb[DR:DR + DS, :].rearrange("n (c t) -> n c t", t=TC))\
                            .then_inc(S["b_stored"], 16)
                    if s == 2:
                        if not last:
                            sp.wait_ge(S["zn_ready"], b * LT + LT)
                            settled(sp, S["passed_sp"])
                            load_x(b + 1)
                        sp.wait_ge(S["ct_ready"], b + 1)
                        settled(sp, S["passed_sp"])
                        for hf in range(2):
                            sp.dma_start(half_view(ct_d, b, hf).rearrange("a p c n -> p (a c) n"),
                                         ct_st[:, hf * CT:(hf + 1) * CT, :]).then_inc(S["ct_stored"], 16)
                    if s == 4:
                        store_ud(b, (0, 1))
                    if s == 5:
                        store_ud(b, (2, 3))
                        store_dd(b, 0)
                    if s == 6:
                        store_gz(b, (0, 1))
                        store_dd(b, 1)
                    if s == 7:
                        store_gz(b, (2, 3))
                        store_dd(b, 2)
                        store_dd(b, 3)

            batch(0)
            with sp.Fori(1, NB - 1) as b:
                batch(b)
            batch(NB - 1, last=True)

            for i in range(2):
                sp.wait_ge(ud_stored[i], NB * LT * 8)
                sp.wait_ge(gz_stored[i], NB * LT * 16)
            sp.wait_ge(S["dd_stored"], NB * ET * 32)
            sp.wait_ge(S["b_stored"], NB * 16)
            sp.wait_ge(S["ct_stored"], NB * 32)
            sp.wait_ge(S["phase_a"], 4)

            def load_dd(c, par):
                sp.dma_start(dd[:, par], dd_d[bass.ds(c, 1)].rearrange("a p k t l -> p (a k) t l"))\
                    .then_inc(dd_loaded[par], 16)
                sp.dma_start(ct[:, par], ct_d[bass.ds(c, 1)].rearrange("a p c n -> p (a c) n"))\
                    .then_inc(dd_loaded[par], 16)

            def load_b(c, g):
                sp.dma_start(b_rows[:, g % 2],
                             b_d[bass.ds(c, 1), g * GR:(g + 1) * GR, :].partition_broadcast(P)
                             .rearrange("p a n t -> p (a n) t")).then_inc(b_loaded[g % 2], 16)

            def load_init(c):
                sp.dma_start(init[:], ud_d[bass.ds(c, 1)].rearrange("a c p e -> p (a c) e"))\
                    .then_inc(S["init_loaded"], 16)

            def load_end(c):
                sp.dma_start(gz[:], gz_d[bass.ds(c, 1)].rearrange("a c p e -> p (a c) e"))\
                    .then_inc(S["gz_loaded"], 16)
                sp.dma_start(x_in[:], x.rearrange("b (v c p) h -> (b v) p c h", p=P, c=CT)[bass.ds(c, 1)]
                             .rearrange("a p c h -> p (a c) h")).then_inc(S["x_loaded"], 16)

            load_dd(0, 0)
            load_b(0, 0)
            load_b(0, 1)
            load_init(0)
            load_end(0)

            def chunk(c, par, more=True, fin=2):
                if more:
                    after(sp, S["exp_done"], c * DS * ET)
                    settled(sp, S["passed_sp"])
                    after(sp, S["db_done"], c * DS)
                    settled(sp, S["passed_sp"])
                    after(sp, S["stt_done"], c * DS * CT)
                    settled(sp, S["passed_sp"])
                    load_dd(c + 1, 1 - par)
                for g in range(2, NG):
                    sp.wait_ge(S["db_done"], c * DS + (g - 1) * GR)
                    settled(sp, S["passed_sp"])
                    load_b(c, g)
                if more:
                    sp.wait_ge(S["stt_done"], c * DS * CT + CT)
                    settled(sp, S["passed_sp"])
                    load_init(c + 1)
                    for g in range(2):
                        sp.wait_ge(S["db_done"], c * DS + (g + NG - 1) * GR)
                        settled(sp, S["passed_sp"])
                        load_b(c + 1, g)

            def store(f):
                for tt in range(CT):
                    sp.wait_ge(S["out_ready"], f * CT + tt + 1)
                    settled(sp, S["passed_sp"])
                    sp.dma_start(out.rearrange("b (v c p) h -> (b v c) p h", p=P, c=CT)[bass.ds(f * CT + tt, 1)]
                                 .rearrange("a p h -> p (a h)"), out_sb[:, tt, :]).then_inc(out_stored[tt], 16)

            def next_end(c):
                sp.wait_ge(S["x1_ready"], (c + 1) * 2)
                settled(sp, S["passed_sp"])
                load_end(c + 1)

            chunk(0, 0)
            chunk(1, 1)
            next_end(0)
            with sp.Fori(1, NCH // 2 - 1) as p:
                for par in range(2):
                    c = p * 2 + par
                    chunk(c, par)
                    next_end(c - 1)
                    store(c - 2)
            chunk(NCH - 2, 0)
            next_end(NCH - 3)
            store(NCH - 4)
            chunk(NCH - 1, 1, more=False)
            next_end(NCH - 2)
            store(NCH - 3)
            store(NCH - 2)
            store(NCH - 1)
            for tt in range(CT):
                sp.wait_ge(out_stored[tt], NCH * 16)

        @block.gpsimd
        def _(pool):
            pool.memset(ident[:], 0.0).then_inc(S["ident_zero"], 1)
            pool.memset(half[:], -0.5).then_inc(S["half_ready"], 1)
            for i in range(2):
                pool.memset(xpad[:, i, 0:KC - 1], 0.0).then_inc(S["pad_zero"], 1)
            pool.wait_ge(S["ident_zero"], 1)
            pool.affine_select(out=ident[:], in_=ident[:], compare_op=ALU.not_equal, fill=1.0, base=0,
                               pattern=[[-1, P]], channel_multiplier=1).then_inc(S["ident_ready"], 1)
            pool.wait_ge(S["half_ready"], 1)
            pool.wait_ge(S["setup"], 1)

            def piece(b, s):
                pool.wait_ge(S["bit0_ready"], b * PIECES + s + 1)
                after(pool, S["level"], b * PIECES + s - 1)
                for j in range(ACT_AFF, NPAIR):
                    settled(pool, S["passed_pool"])
                    pool.tensor_scalar(pair[:, s % 2, j, :], bit0[:, s % 2, :], lut_d[:, j:j + 1],
                                       lut_s[:, 2 * j:2 * j + 1], ALU.mult, ALU.add).then_inc(S["pairs_pool"], 1)

            def low_part(b, s):
                pool.wait_ge(S["whi_ready"], b * PIECES + s + 1)
                cols = bass.ds(b * (PIECES * PW) + s * PW, PW)
                pool.tensor_tensor(w_lo[:, cols], pair[:, s % 2, 0, :], w_hi[:, cols], ALU.subtract)\
                    .then_inc(S["wlo_ready"], 1)

            def z_scales(b):
                pool.wait_ge(S["zstat"], b * 6 + 6)
                after(pool, S["zn_ready"], b * LT)
                pool.tensor_tensor(zsc[:, 2, :], zsc[:, 0, :], half[:], ALU.pow).then_inc(S["zpow"], 1)
                pool.wait_ge(S["zpow"], b * 2 + 1)
                settled(pool, S["passed_pool"])
                pool.tensor_scalar(zsc[:, 3, :], zsc[:, 2, :], 0.5, 1.0, ALU.mult, ALU.mult)\
                    .then_inc(S["zpow"], 1)

            def z_half(b):
                pool.wait_ge(S["zpow"], b * 2 + 2)
                after(pool, S["gzt_ready"], b * LT)
                for st in range(LT):
                    settled(pool, S["passed_pool"])
                    pool.tensor_scalar(zn[:, st, :], x_sb[:, st, :], zsc[:, 1, st:st + 1], zsc[:, 3, st:st + 1],
                                       ALU.add, ALU.mult).then_inc(S["zn_ready"], 1)

            def one_plus(b, et):
                pool.wait_ge(S["eexp_ready"], b * ET + et + 1)
                after(pool, S["dd_stored"], b * (ET * 32))
                settled(pool, S["passed_pool"])
                pool.tensor_scalar(e_ln[:, et, :], e_exp[:, et, :], 1.0, 1.0, ALU.add, ALU.mult)\
                    .then_inc(S["w_ready"], 1)

            def delta(b, et):
                pool.wait_ge(S["ln_ready"], b * ET + et + 1)
                pool.tensor_tensor(e_ln[:, et, :], e_ln[:, et, :], e_exp[:, et, :], ALU.subtract)\
                    .then_inc(S["delta_ready"], 1)
                pool.wait_ge(S["delta_ready"], b * (2 * ET) + 2 * et + 1)
                pool.tensor_tensor(e_relu[:, et, :], e_ln[:, et, :], e_relu[:, et, :], ALU.add)\
                    .then_inc(S["delta_ready"], 1)
                pool.wait_ge(S["delta_ready"], b * (2 * ET) + 2 * et + 2)
                pool.tensor_tensor(e_ln[:, et, :], e_relu[:, et, :], u_sb[:, et, :], ALU.mult)\
                    .then_inc(S["sp_ready"], 1)

            def batch(b, last=False):
                for s in range(PIECES):
                    if s or not isinstance(b, int) or b:
                        low_part(b, s - 1)
                    if not (last and s == PIECES - 1):
                        piece(b, s + 1)
                    if s == 0:
                        z_scales(b)
                    if s == 1:
                        z_half(b)
                    if s in (2, 3):
                        one_plus(b, 2 * s - 4)
                        one_plus(b, 2 * s - 3)
                    if s >= 4:
                        delta(b, s - 4)

            piece(0, 0)
            batch(0)
            with pool.Fori(1, NB - 1) as b:
                batch(b)
            batch(NB - 1, last=True)
            low_part(NB - 1, PIECES - 1)

            pool.wait_ge(S["wlo_ready"], NB * PIECES)
            pool.sem_inc(S["phase_a"], 1)
            pool.wait_ge(S["phase_a"], 4)

            def state(c, par, n):
                if n == 0:
                    pool.wait_ge(dd_loaded[par], c * 16 + (32 if par == 0 else 16))
                if n % GR == 0:
                    g = n // GR
                    pool.wait_ge(b_loaded[g % 2], c * (NG // 2 * 16) + 16 * (g // 2 + 1))
                after(pool, S["scan_done"], c * (DS * ET) + (n - 1) * ET)
                pool.tensor_tensor(
                    db[:, n % 2], dd[:, par, 1], b_rows[:, (n // GR) % 2, n % GR:n % GR + 1, :].to_broadcast([P, ET, TC]),
                    ALU.mult).then_inc(S["db_done"], 1)

            def normal(f):
                pool.wait_ge(S["fin_stat"], f * 4 + 4)
                after(pool, S["xn_ready"], f * CT)
                pool.tensor_tensor(nsc[:, 2, :], nsc[:, 0, :], half[:, 0:CT], ALU.pow).then_inc(S["npow"], 1)
                pool.wait_ge(S["npow"], f * 2 + 1)
                settled(pool, S["passed_pool"])
                pool.tensor_scalar(nsc[:, 3, :], nsc[:, 2, :], 256.0, 1.0, ALU.mult, ALU.mult)\
                    .then_inc(S["npow"], 1)
                pool.wait_ge(S["npow"], f * 2 + 2)
                after(pool, S["xnt_ready"], f * 2)

            def normal_rows(f, par):
                for tt in range(CT):
                    settled(pool, S["passed_pool"])
                    pool.tensor_scalar(xn[:, tt, :], x1[:, par, tt, :], nsc[:, 1, tt:tt + 1], nsc[:, 3, tt:tt + 1],
                                       ALU.add, ALU.mult).then_inc(S["xn_ready"], 1)

            def gated(f, g):
                two = 2 if g < JT // 2 else 1
                rp = rows(2 * g)
                slot = g % 2
                pool.wait_ge(S["q_ready"], f * JT + 2 * g + two)
                pool.wait_ge(S["us_ready"], f * JT + 2 * g + two)
                pool.tensor_tensor(u_gate[0:rp, slot, 0:two, :], q_gate[0:rp, slot, 0:two, :],
                                   u_gate[0:rp, slot, 0:two, :], ALU.mult).then_inc(S["hs_ready"], 1)

            def gated_low(f, g):
                two = 2 if g < JT // 2 else 1
                rp = rows(2 * g)
                slot = g % 2
                pool.wait_ge(S["hhi_ready"], f * 6 + g + 1)
                if g == 0:
                    after(pool, S["dn_ready"], f * CT)
                pool.tensor_tensor(h_lo[0:rp, 2 * g:2 * g + two, :], u_gate[0:rp, slot, 0:two, :],
                                   h_hi[0:rp, 2 * g:2 * g + two, :], ALU.subtract).then_inc(S["hlo_ready"], 1)

            def chunk(c, par, ssm, ffn):
                for n in range(DS):
                    if ssm:
                        state(c, par, n)
                    if ffn:
                        if n == 0:
                            normal(c - 1)
                            normal_rows(c - 1, 1 - par)
                        if n >= 6 and n % 2 == 0:
                            gated(c - 1, (n - 6) // 2)
                            if n >= 8:
                                gated_low(c - 1, (n - 8) // 2)
                        if n == DS - 1:
                            gated(c - 1, 5)
                            gated_low(c - 1, 4)
                            gated_low(c - 1, 5)

            chunk(0, 0, True, False)
            chunk(1, 1, True, True)
            with pool.Fori(1, NCH // 2) as p:
                for par in range(2):
                    chunk(p * 2 + par, par, True, True)
            chunk(NCH, 0, False, True)

        @block.scalar
        def _(act):
            act.wait_ge(S["vec_loaded"], 80)
            act.activation(neg_a[:], neg_a[:], ACT.Exp).then_inc(S["setup_act"], 1)
            act.mul(cb_half[:], vec[:, 0, :], 0.5).then_inc(S["setup_act"], 1)
            act.wait_ge(S["setup_act"], 2)
            act.mul(neg_a[:], neg_a[:], -1.0).then_inc(S["setup_act"], 1)
            act.wait_ge(S["pad_zero"], 2)
            act.wait_ge(S["setup"], 1)
            act.wait_ge(S["setup_act"], 3)

            def piece(b, s):
                act.wait_ge(S["bit0_ready"], b * PIECES + s + 1)
                after(act, S["level"], b * PIECES + s - 1)
                for j in reversed(range(ACT_AFF)):
                    if j == 0:
                        after(act, S["wlo_ready"], b * PIECES + s - 1)
                    act.activation(pair[:, s % 2, j, :], bit0[:, s % 2, :], ACT.Identity, scale=lut_d[:, j:j + 1],
                                   bias=lut_s[:, 2 * j:2 * j + 1]).then_inc(S["pairs_act"], 1)

            def high_part(b, s):
                act.wait_ge(S["level"], b * PIECES + s + 1)
                act.copy(w_hi[:, bass.ds(b * (PIECES * PW) + s * PW, PW)], pair[:, s % 2, 0, :])\
                    .then_inc(S["whi_ready"], 1)

            def pad(b, et):
                act.wait_ge(S["xp_ready"], b * ET + et + 1)
                after(act, S["v_ready"], b * ET + max(et - 1, 0))
                act.copy(xpad[:, et % 2, KC - 1:], bank[et % 2][:]).then_inc(S["xpad_ready"], 1)

            def gate_u(b, et):
                act.wait_ge(S["v_ready"], b * ET + et + 1)
                after(act, S["u_ready"], b * ET + max(et - 1, 0))
                if et < 2:
                    after(act, S["gz_ready"], b * LT)
                act.activation(v_half[:, et % 2, :], bank[2 + et % 2][:], ACT.Identity, scale=0.5,
                               bias=cb_half[:, et:et + 1]).then_inc(S["vhalf_ready"], 1)
                act.activation(v_tanh[:, et % 2, :], bank[2 + et % 2][:], ACT.Tanh, scale=0.5,
                               bias=cb_half[:, et:et + 1]).then_inc(S["vhalf_ready"], 1)

            def z_tanh(b, st):
                act.wait_ge(S["zn_ready"], b * LT + st + 1)
                if st < 2:
                    act.wait_ge(S["u_ready"], b * ET + ET)
                else:
                    act.wait_ge(S["gz_ready"], b * LT + st - 1)
                act.activation(v_tanh[:, st % 2, :], zn[:, st, :], ACT.Tanh).then_inc(S["ztanh_ready"], 1)

            def low_rank(b):
                act.wait_ge(S["xdbl_ready"], b + 1)
                after(act, S["b_stored"], b * 16)
                after(act, S["ctt_ready"], b)
                act.copy(xdbl_sb[:], bank[4][0:NX, :]).then_inc(S["xdbl_sb_ready"], 1)

            def soft(b, et):
                act.wait_ge(S["dt_ready"], b * ET + et + 1)
                if et == 0:
                    after(act, S["sp_ready"], b * ET)
                    after(act, S["dd_stored"], b * (ET * 32))
                act.activation(e_exp[:, et, :], bank[et % 2][:], ACT.Abs, bias=vec[:, 1, et:et + 1])\
                    .then_inc(S["eabs_ready"], 1)
                act.activation(e_relu[:, et, :], bank[et % 2][:], ACT.Relu, bias=vec[:, 1, et:et + 1])\
                    .then_inc(S["erelu_ready"], 1)
                act.wait_ge(S["eabs_ready"], b * ET + et + 1)
                act.activation(e_exp[:, et, :], e_exp[:, et, :], ACT.Exp, scale=-1.0)\
                    .then_inc(S["eexp_ready"], 1)

            def log(b, et):
                act.wait_ge(S["t_ready"], b * ET + et + 1)
                act.activation(e_ln[:, et, :], e_ln[:, et, :], ACT.Ln).then_inc(S["ln_ready"], 1)

            def c_rows(b):
                act.wait_ge(S["ctt_ready"], b + 1)
                after(act, S["ct_stored"], b * 32)
                act.copy(ct_st[:], bank[5][:, 0:LT * NX].rearrange("p (t k) -> p t k", k=NX)[:, :, DR + DS:NX])\
                    .then_inc(S["ct_ready"], 1)

            def ud_out(b, tt):
                act.wait_ge(S["ud_ready"], b * LT + tt + 1)
                after(act, ud_stored[tt % 2], b * 32 + 16 * (tt // 2))
                act.copy(ud_st[:, tt % 2, :], bank[6 + tt % 2][:]).then_inc(S["ud_free"], 1)

            def gz_out(b, st):
                act.wait_ge(S["gzt_ready"], b * LT + st + 1)
                after(act, gz_stored[st % 2], b * 64 + 32 * (st // 2))
                act.copy(gz_st[:, st % 2], bank[6 + st % 2][:].rearrange("p (l s) -> p l s", s=P))\
                    .then_inc(S["gz_st_ready"], 1)

            def batch(b, last=False):
                for s in range(PIECES):
                    if s == 1:
                        low_rank(b)
                    if s or not isinstance(b, int) or b:
                        high_part(b, s - 1)
                    if not (last and s == PIECES - 1):
                        piece(b, s + 1)
                    if s == 0:
                        gate_u(b, 2)
                        gate_u(b, 3)
                    if s in (1, 2):
                        soft(b, 2 * s - 2)
                        soft(b, 2 * s - 1)
                    if s == 2:
                        c_rows(b)
                    if s == 3:
                        z_tanh(b, 0)
                        z_tanh(b, 1)
                        log(b, 0)
                        log(b, 1)
                    if s == 4:
                        log(b, 2)
                        log(b, 3)
                        z_tanh(b, 2)
                        z_tanh(b, 3)
                        ud_out(b, 0)
                        ud_out(b, 1)
                    if s == 5:
                        ud_out(b, 2)
                        ud_out(b, 3)
                        if not last:
                            pad(b + 1, 0)
                            pad(b + 1, 1)
                        gz_out(b, 0)
                        gz_out(b, 1)
                    if s == 6:
                        if not last:
                            pad(b + 1, 2)
                            pad(b + 1, 3)
                        gz_out(b, 2)
                        gz_out(b, 3)
                    if s == 7 and not last:
                        gate_u(b + 1, 0)
                        gate_u(b + 1, 1)

            piece(0, 0)
            for et in range(ET):
                pad(0, et)
            gate_u(0, 0)
            gate_u(0, 1)
            batch(0)
            with act.Fori(1, NB - 1) as b:
                batch(b)
            batch(NB - 1, last=True)
            high_part(NB - 1, PIECES - 1)

            act.wait_ge(S["whi_ready"], NB * PIECES)
            act.sem_inc(S["phase_a"], 1)
            act.wait_ge(S["phase_a"], 4)

            def decay(c, par, n):
                if n == 0:
                    act.wait_ge(dd_loaded[par], c * 16 + (32 if par == 0 else 16))
                for et in range(ET):
                    if et % 2 == 0:
                        after(act, S["scan_done"], c * (DS * ET) + (n - 1) * ET + et + 2)
                    act.activation(bank[2 + et // 2][:, (et % 2) * TC:(et % 2 + 1) * TC], dd[:, par, 0, et, :],
                                   ACT.Exp, scale=neg_a[:, et, n:n + 1]).then_inc(S["exp_done"], 1)

            def high_x(f):
                for k in range(2):
                    act.wait_ge(S["xnt_ready"], f * 2 + k + 1)
                    if k == 0:
                        after(act, S["gu_ready"], f * JT)
                    act.copy(xt_hi[:, 2 * k:2 * k + 2, :], bank[4 + k][:].rearrange("p (a t) -> p a t", t=TC))\
                        .then_inc(S["xhi_ready"], 1)

            def gate(f, j):
                r = rows(j)
                act.wait_ge(S["gu_ready"], f * JT + j + 1)
                after(act, S["q_ready"], f * JT + j - 1)
                act.activation(g_tanh[0:r, j % 2, :], bank[4 + j % 2][0:r, 0:TC], ACT.Tanh,
                               scale=tanh_scale[0:r, :]).then_inc(S["gt_ready"], 1)
                if j % 2 == 0:
                    after(act, S["hlo_ready"], f * 6 + max(j // 2 - 1, 0))
                act.activation(u_gate[0:r, (j // 2) % 2, j % 2, :], bank[4 + j % 2][0:r, TC:2 * TC], ACT.Identity,
                               scale=2.0 ** -42).then_inc(S["us_ready"], 1)

            def high_h(f, g):
                two = 2 if g < JT // 2 else 1
                rp = rows(2 * g)
                act.wait_ge(S["hs_ready"], f * 6 + g + 1)
                if g == 0:
                    after(act, S["dn_ready"], f * CT)
                act.copy(h_hi[0:rp, 2 * g:2 * g + two, :], u_gate[0:rp, g % 2, 0:two, :])\
                    .then_inc(S["hhi_ready"], 1)

            def chunk(c, par, ssm, ffn):
                f = c - 1
                for n in range(DS):
                    if ssm:
                        decay(c, par, n)
                    if ffn:
                        if n == 1:
                            high_x(f)
                        if n > GU0 and n - GU0 - 1 < JT:
                            gate(f, n - GU0 - 1)
                        if n >= 7 and n % 2 == 1:
                            high_h(f, (n - 7) // 2)
                        if n == DS - 1:
                            high_h(f, 5)

            chunk(0, 0, True, False)
            chunk(1, 1, True, True)
            with act.Fori(1, NCH // 2) as p:
                for par in range(2):
                    chunk(p * 2 + par, par, True, True)
            chunk(NCH, 0, False, True)

        @block.vector
        def _(dve):
            step = S["picked"]
            dve.wait_ge(S["lut_loaded"], 16)
            dve.tensor_reduce(sc[:, 2:3], lut_in[:], AX.X, ALU.max, apply_absolute_value=True).then_inc(step, 1)
            dve.wait_ge(step, 1)
            dve.tensor_scalar(sc[:, 3:4], sc[:, 2:3], 1e-12, None, ALU.max).then_inc(step, 1)
            dve.wait_ge(step, 2)
            dve.tensor_scalar(lut_i[:, 0:1], sc[:, 3:4].bitcast(I32), 0x7F800000, None, ALU.bitwise_and)\
                .then_inc(step, 1)
            dve.wait_ge(step, 3)
            dve.tensor_scalar(lut_i[:, 1:2], lut_i[:, 0:1], -1.0, float(0x7F000000), ALU.mult, ALU.add)\
                .then_inc(step, 1)
            dve.wait_ge(step, 4)
            dve.tensor_scalar(lut_s[:], lut_in[:], lut_i[:, 1:2].bitcast(F32), 2.0 ** 10, ALU.mult, ALU.mult)\
                .then_inc(step, 1)
            dve.tensor_scalar(tanh_scale, lut_i[:, 0:1].bitcast(F32), 2.0 ** -19, None, ALU.mult)\
                .then_inc(step, 1)
            dve.tensor_scalar(sc[:, 4:5], lut_i[:, 0:1].bitcast(F32), lut_i[:, 0:1].bitcast(F32), None, ALU.mult)\
                .then_inc(step, 1)
            dve.wait_ge(step, 7)
            dve.tensor_scalar(out_scale, sc[:, 4:5], lut_i[:, 0:1].bitcast(F32), 2.0 ** -5, ALU.mult, ALU.mult)\
                .then_inc(step, 1)
            pairs = lut_s[:].rearrange("p (j two) -> p j two", two=2)
            dve.tensor_tensor(lut_d[:], pairs[:, :, 1], pairs[:, :, 0], ALU.subtract).then_inc(step, 1)
            dve.wait_ge(step, 9)
            dve.sem_inc(S["setup"], 1)
            dve.wait_ge(S["vec_loaded"], 80)
            dve.wait_ge(S["ident_ready"], 1)
            for et in range(ET):
                for k in range(KC):
                    dve.tensor_scalar(conv_diag[:, et, k, :], ident[:], cw_sb[:, et, k:k + 1], None, ALU.mult)\
                        .then_inc(S["setup"], 1)
                dve.tensor_scalar(d_diag[:, et, :], ident[:], vec[:, 2, et:et + 1], None, ALU.mult)\
                    .then_inc(S["setup"], 1)

            def lowest_bit(b, s):
                dve.wait_ge(idx_loaded[s % 2], b * (PIECES * 8) + 16 * (s // 2) + 16)
                after(dve, S["pairs_act"], b * (PIECES * ACT_AFF) + (s - 1) * ACT_AFF)
                after(dve, S["pairs_pool"], b * (PIECES * (NPAIR - ACT_AFF)) + (s - 1) * (NPAIR - ACT_AFF))
                dve.tensor_scalar(bit0[:, s % 2, :], idx_sb[:, s % 2, :], 1, None, ALU.bitwise_and)\
                    .then_inc(S["bit0_ready"], 1)

            def masks(b, s):
                after(dve, S["level"], b * PIECES + s)
                for i in range(3):
                    m = dve.tensor_scalar(bits[:, i, :], idx_sb[:, s % 2, :], 2 << i, None, ALU.bitwise_and)
                m.then_inc(S["masks_ready"], 1)

            def select(b, s):
                dve.wait_ge(S["masks_ready"], b * PIECES + s + 1)
                dve.wait_ge(S["pairs_act"], b * (PIECES * ACT_AFF) + (s + 1) * ACT_AFF)
                dve.wait_ge(S["pairs_pool"], b * (PIECES * (NPAIR - ACT_AFF)) + (s + 1) * (NPAIR - ACT_AFF))
                for i, inc in ((0, S["picked"]), (1, S["picked"]), (2, S["level"])):
                    k = NPAIR >> (i + 1)
                    dst = pair[:, s % 2].rearrange("p (k two r) w -> p k two r w", two=2, r=1 << i)
                    if i:
                        dve.wait_ge(S["picked"], b * (2 * PIECES) + (9 + 2 * s + i))
                    settled(dve, S["passed_dve"])
                    dve.copy_predicated(dst[:, :, 0, 0, :], bits[:, i:i + 1, :].to_broadcast([P, k, PW]),
                                        dst[:, :, 1, 0, :]).then_inc(inc, 1)

            def z_stats(b):
                dve.wait_ge(S["xa_loaded"], b * 16 + 16)
                for st in range(LT):
                    dve.bn_stats(stats[:, st, :], x_sb[:, st, :]).then_inc(S["zstat"], 1)
                dve.wait_ge(S["zstat"], b * 6 + 4)
                settled(dve, S["passed_dve"])
                for st in range(LT):
                    m = dve.bn_aggr(mv[:, st, :], stats[:, st, :])
                m.then_inc(S["zsc_ready"], 1)
                dve.wait_ge(S["zsc_ready"], b + 1)
                after(dve, S["zn_ready"], b * LT)
                dve.tensor_scalar(zsc[:, 0, :], mv[:, :, 1], EPS, None, ALU.add).then_inc(S["zstat"], 1)
                dve.tensor_scalar(zsc[:, 1, :], mv[:, :, 0], -1.0, None, ALU.mult).then_inc(S["zstat"], 1)

            def silu_u(b, et):
                dve.wait_ge(S["vhalf_ready"], b * (2 * ET) + 2 * et + 2)
                if et == 0:
                    after(dve, S["sp_ready"], b * ET)
                    after(dve, S["ud_ready"], b * LT)
                dve.scalar_tensor_tensor(u_sb[:, et, :], v_tanh[:, et % 2, :], 1.0, v_half[:, et % 2, :],
                                         ALU.add, ALU.mult).then_inc(S["u_ready"], 1)

            def silu_z(b, st):
                dve.wait_ge(S["ztanh_ready"], b * LT + st + 1)
                dve.scalar_tensor_tensor(zn[:, st, :], v_tanh[:, st % 2, :], 1.0, zn[:, st, :],
                                         ALU.add, ALU.mult).then_inc(S["gz_ready"], 1)

            def lost(b, et):
                dve.wait_ge(S["w_ready"], b * ET + et + 1)
                dve.scalar_tensor_tensor(e_exp[:, et, :], e_ln[:, et, :], 1.0, e_exp[:, et, :],
                                         ALU.subtract, ALU.subtract).then_inc(S["t_ready"], 1)

            def batch(b, last=False):
                for s in range(PIECES):
                    if not (last and s == PIECES - 1):
                        lowest_bit(b, s + 1)
                    masks(b, s)
                    if s == 0:
                        silu_u(b, 0)
                        silu_u(b, 1)
                    if s == 3:
                        lost(b, 0)
                        lost(b, 1)
                    select(b, s)
                    if s == 0:
                        silu_u(b, 2)
                        silu_u(b, 3)
                    if s == 3:
                        lost(b, 2)
                        lost(b, 3)
                    if s in (4, 5):
                        silu_z(b, 2 * s - 8)
                        silu_z(b, 2 * s - 7)
                    if s == 6 and not last:
                        z_stats(b + 1)

            lowest_bit(0, 0)
            z_stats(0)
            batch(0)
            with dve.Fori(1, NB - 1) as b:
                batch(b)
            batch(NB - 1, last=True)

            dve.wait_ge(S["level"], NB * PIECES)
            dve.wait_ge(S["setup"], 1 + ET * (KC + 1))
            dve.sem_inc(S["phase_a"], 1)
            dve.wait_ge(S["phase_a"], 4)

            def scans(c, par, n):
                dve.wait_ge(S["db_done"], c * DS + n + 1)
                after(dve, S["ht_ready"], c * (DS * CT) + (n - 1) * CT)
                if par == 0:
                    after(dve, S["hl_saved"], (c * (DS // 2) + n - 1) if n else c * (DS // 2))
                elif n < 2:
                    dve.wait_ge(S["hl_saved"], c * (DS // 2) + (DS // 2 - 1) + n)
                for et in range(ET):
                    if et % 2 == 0:
                        dve.wait_ge(S["exp_done"], c * (DS * ET) + n * ET + et + 2)
                    first = 0.0 if par == 0 else h_last[:, n, et:et + 1]
                    dve.tensor_tensor_scan(h[:, n % 2, et, :],
                                           bank[2 + et // 2][:, (et % 2) * TC:(et % 2 + 1) * TC],
                                           db[:, n % 2, et, :], first, ALU.mult, ALU.add)\
                        .then_inc(S["scan_done"], 1)

            def outputs(c, par, n):
                for tt in range(CT):
                    dve.wait_ge(S["ht_ready"], c * (DS * CT) + n * CT + tt + 1)
                    if n == 0:
                        if tt == 0:
                            dve.wait_ge(S["init_loaded"], c * 16 + 16)
                            after(dve, S["x1_ready"], c * 2)
                        base = init
                    else:
                        dve.wait_ge(S["stt_done"], c * (DS * CT) + (n - 1) * CT + tt + 1)
                        base = acc
                    dve.scalar_tensor_tensor(acc[:, tt, :], bank[tt][:], ct[:, par, tt, n:n + 1], base[:, tt, :],
                                             ALU.mult, ALU.add).then_inc(S["stt_done"], 1)
                if par == 0:
                    dve.wait_ge(S["scan_done"], c * (DS * ET) + (n + 1) * ET)
                    dve.tensor_copy(h_last[:, n, :], h[:, n % 2, :, TC - 1]).then_inc(S["hl_saved"], 1)

            def finish(c, par):
                dve.wait_ge(S["stt_done"], (c + 1) * (DS * CT))
                dve.wait_ge(S["gz_loaded"], c * 16 + 16)
                dve.tensor_tensor(x1[:, par], acc[:], gz[:], ALU.mult).then_inc(S["x1_ready"], 1)
                dve.wait_ge(S["x_loaded"], c * 16 + 16)
                dve.wait_ge(S["x1_ready"], c * 2 + 1)
                dve.tensor_tensor(x1[:, par], x1[:, par], x_in[:], ALU.add).then_inc(S["x1_ready"], 1)
                dve.wait_ge(S["x1_ready"], c * 2 + 2)
                for tt in range(CT):
                    m = dve.bn_stats(stats2[:, tt, :], x1[:, par, tt, :])
                m.then_inc(S["fin_stat"], 1)
                dve.wait_ge(S["fin_stat"], c * 4 + 1)
                settled(dve, S["passed_dve"])
                for tt in range(CT):
                    m = dve.bn_aggr(mv2[:, tt, :], stats2[:, tt, :])
                m.then_inc(S["fin_stat"], 1)
                dve.wait_ge(S["fin_stat"], c * 4 + 2)
                after(dve, S["xn_ready"], c * CT)
                dve.tensor_scalar(nsc[:, 0, :], mv2[:, :, 1], EPS, None, ALU.add).then_inc(S["fin_stat"], 1)
                dve.tensor_scalar(nsc[:, 1, :], mv2[:, :, 0], -1.0, None, ALU.mult).then_inc(S["fin_stat"], 1)

            def low_x(f):
                for k in range(2):
                    dve.wait_ge(S["xhi_ready"], f * 2 + k + 1)
                    if k == 0:
                        after(dve, S["gu_ready"], f * JT)
                    dve.tensor_tensor(xt_lo[:, 2 * k:2 * k + 2, :], bank[4 + k][:].rearrange("p (a t) -> p a t", t=TC),
                                      xt_hi[:, 2 * k:2 * k + 2, :], ALU.subtract).then_inc(S["xlo_ready"], 1)

            def gate(f, j):
                r = rows(j)
                dve.wait_ge(S["us_ready"], f * JT + j + 1)
                if j % 2 == 0:
                    after(dve, S["hs_ready"], f * 6 + max(j // 2 - 1, 0))
                dve.scalar_tensor_tensor(q_gate[0:r, (j // 2) % 2, j % 2, :], g_tanh[0:r, j % 2, :], 1.0,
                                         bank[4 + j % 2][0:r, 0:TC], ALU.add, ALU.mult).then_inc(S["q_ready"], 1)

            def result(f, par, tt):
                dve.wait_ge(S["dn_ready"], f * CT + tt + 1)
                after(dve, out_stored[tt], f * 16)
                dve.scalar_tensor_tensor(out_sb[:, tt, :], bank[6 + tt][:], out_scale, x1[:, par, tt, :],
                                         ALU.mult, ALU.add).then_inc(S["out_ready"], 1)

            def chunk(c, par, ssm, ffn, down):
                f = c - 1
                for n in range(DS):
                    if ssm:
                        scans(c, par, n)
                        if n:
                            outputs(c, par, n - 1)
                    if n == 0 and ffn:
                        outputs(f, 1 - par, DS - 1)
                        finish(f, 1 - par)
                    if down and n in (1, 2):
                        result(c - 2, par, n - 1)
                    if ffn:
                        if n == 1:
                            low_x(f)
                        if n > GU0 and n - GU0 - 1 < JT:
                            gate(f, n - GU0 - 1)

            chunk(0, 0, True, False, False)
            chunk(1, 1, True, True, False)
            with dve.Fori(1, NCH // 2) as p:
                for par in range(2):
                    chunk(p * 2 + par, par, True, True, True)
            chunk(NCH, 0, False, True, True)
            for tt in range(CT):
                result(NCH - 1, 1, tt)

        @block.tensor
        def _(pe):
            pe.wait_ge(S["params_loaded"], 48)
            pe.wait_ge(S["ident_ready"], 1)
            pe.wait_ge(S["setup"], 1 + ET * (KC + 1))

            def in_proj(b, et):
                after(pe, S["xpad_ready"], b * ET + max(et - 1, 0))
                if et < 2:
                    after(pe, S["eexp_ready"], b * ET)
                    after(pe, S["erelu_ready"], b * ET)
                for k in range(KM):
                    m = pe.matmul(bank[et % 2][:], win_sb[:, k, et * P:(et + 1) * P], ctx_sb[:, k, :],
                                  start=(k == 0), stop=(k == KM - 1))
                m.then_inc(S["xp_ready"], 1)

            def conv(b, et):
                pe.wait_ge(S["xpad_ready"], b * ET + et + 1)
                after(pe, S["vhalf_ready"], b * (2 * ET) + 2 * max(et - 1, 0))
                for k in range(KC):
                    m = pe.matmul(bank[2 + et % 2][:], conv_diag[:, et, k, :], xpad[:, et % 2, k:k + L],
                                  start=(k == 0), stop=(k == KC - 1))
                m.then_inc(S["v_ready"], 1)

            def low_rank(b):
                after(pe, S["xdbl_sb_ready"], b)
                for et in range(ET):
                    pe.wait_ge(S["u_ready"], b * ET + et + 1)
                    m = pe.matmul(bank[4][0:NX, :], xproj_sb[:, et, :], u_sb[:, et, :],
                                  start=(et == 0), stop=(et == ET - 1))
                m.then_inc(S["xdbl_ready"], 1)
                pe.wait_ge(S["xdbl_sb_ready"], b + 1)
                for et in range(ET):
                    if et >= 2:
                        pe.wait_ge(S["eexp_ready"], b * ET + et - 1)
                        pe.wait_ge(S["erelu_ready"], b * ET + et - 1)
                    else:
                        pe.wait_ge(S["xpad_ready"], b * ET + ET)
                    pe.matmul(bank[et % 2][:], dt_sb[:, et * P:(et + 1) * P], xdbl_sb[0:DR, :],
                              start=True, stop=True).then_inc(S["dt_ready"], 1)
                after(pe, S["ct_ready"], b)
                settled(pe, S["passed_pe"])
                for tt in range(LT):
                    m = pe.transpose(bank[5][:, tt * NX:(tt + 1) * NX], xdbl_sb[:, tt * P:(tt + 1) * P],
                                     ident[0:NX, 0:NX])
                m.then_inc(S["ctt_ready"], 1)

            def skip_part(b, tt):
                if tt < 2:
                    after(pe, S["gz_st_ready"], b * LT)
                else:
                    pe.wait_ge(S["ud_free"], b * LT + tt - 1)
                for et in range(ET):
                    m = pe.matmul(bank[6 + tt % 2][:, et * P:(et + 1) * P], u_sb[:, et, tt * P:(tt + 1) * P],
                                  d_diag[:, et, :], start=True, stop=True)
                m.then_inc(S["ud_ready"], 1)

            def gate_part(b, st):
                pe.wait_ge(S["gz_ready"], b * LT + st + 1)
                if st < 2:
                    pe.wait_ge(S["ud_free"], b * LT + st + 3)
                else:
                    pe.wait_ge(S["gz_st_ready"], b * LT + st - 1)
                for lt in range(LT):
                    m = pe.transpose(bank[6 + st % 2][:, lt * P:(lt + 1) * P], zn[:, st, lt * P:(lt + 1) * P],
                                     ident[:])
                m.then_inc(S["gzt_ready"], 1)

            def batch(b, last=False):
                low_rank(b)
                for tt in range(LT):
                    skip_part(b, tt)
                if not last:
                    pe.wait_ge(S["ctx_loaded"], b * 16 + 32)
                    in_proj(b + 1, 0)
                    in_proj(b + 1, 1)
                gate_part(b, 0)
                gate_part(b, 1)
                if not last:
                    conv(b + 1, 0)
                    conv(b + 1, 1)
                    in_proj(b + 1, 2)
                    in_proj(b + 1, 3)
                gate_part(b, 2)
                gate_part(b, 3)
                if not last:
                    conv(b + 1, 2)
                    conv(b + 1, 3)

            pe.wait_ge(S["ctx_loaded"], 16)
            in_proj(0, 0)
            in_proj(0, 1)
            conv(0, 0)
            conv(0, 1)
            in_proj(0, 2)
            in_proj(0, 3)
            conv(0, 2)
            conv(0, 3)
            batch(0)
            with pe.Fori(1, NB - 1) as b:
                batch(b)
            batch(NB - 1, last=True)

            pe.wait_ge(S["ud_free"], NB * LT)
            pe.wait_ge(S["gz_st_ready"], NB * LT)
            pe.wait_ge(S["ct_ready"], NB)
            pe.wait_ge(S["eexp_ready"], NB * ET)
            pe.wait_ge(S["gzt_ready"], NB * LT)
            pe.sem_inc(S["phase_a"], 1)
            pe.wait_ge(S["phase_a"], 4)

            def turn(c, n):
                for tt in range(CT):
                    after(pe, S["stt_done"], c * (DS * CT) + (n - 1) * CT + tt + 1)
                    for et in range(ET):
                        if tt == 0:
                            pe.wait_ge(S["scan_done"], c * (DS * ET) + n * ET + et + 1)
                        m = pe.transpose(bank[tt][:, et * P:(et + 1) * P], h[:, n % 2, et, tt * P:(tt + 1) * P],
                                         ident[:])
                    m.then_inc(S["ht_ready"], 1)

            def turn_x(f):
                for k in range(2):
                    after(pe, S["q_ready"], f * JT)
                    after(pe, S["us_ready"], f * JT)
                    pe.wait_ge(S["xn_ready"], f * CT + CT)
                    for a in range(2):
                        for tt in range(CT):
                            kt = 2 * k + a
                            m = pe.transpose(bank[4 + k][:, a * TC + tt * P:a * TC + (tt + 1) * P],
                                             xn[:, tt, kt * P:(kt + 1) * P], ident[:])
                    m.then_inc(S["xnt_ready"], 1)

            def gate_up(f, j):
                r = rows(j)
                if j == 0:
                    pe.wait_ge(S["xlo_ready"], f * 2 + 2)
                else:
                    after(pe, S["q_ready"], f * JT + j - 1)
                    after(pe, S["us_ready"], f * JT + j - 1)
                for part, w0 in ((0, 0), (TC, UP0)):
                    i = 0
                    for kt in range(KT):
                        cols = slice(w0 + kt * INTER + j * P, w0 + kt * INTER + j * P + r)
                        for w, v in ((w_hi, xt_hi), (w_hi, xt_lo), (w_lo, xt_hi)):
                            m = pe.matmul(bank[4 + j % 2][0:r, part:part + TC], w[:, cols], v[:, kt, :],
                                          start=(i == 0), stop=(i == 3 * KT - 1))
                            i += 1
                m.then_inc(S["gu_ready"], 1)

            def down(f, part):
                for tt, j in down_parts[part]:
                    r = rows(j)
                    if j % 2 == 0 and tt == 0:
                        pe.wait_ge(S["hlo_ready"], f * 6 + j // 2 + 1)
                    if j == 0:
                        after(pe, S["out_ready"], f * CT - CT + tt + 1)
                    cols = slice(DN0 + j * HID, DN0 + (j + 1) * HID)
                    toks = slice(tt * P, (tt + 1) * P)
                    for i, (v, w) in enumerate(((h_hi, w_hi), (h_hi, w_lo), (h_lo, w_hi))):
                        m = pe.matmul(bank[6 + tt][:], v[0:r, j, toks], w[0:r, cols],
                                      start=(j == 0 and i == 0), stop=(j == JT - 1 and i == 2))
                    if j == JT - 1:
                        m.then_inc(S["dn_ready"], 1)

            def chunk(c, ssm, ffn, rest):
                f = c - 1
                for n in range(DS):
                    if rest and n < 2:
                        down(c - 2, 2 + n)
                    if ssm:
                        turn(c, n)
                    if ffn:
                        if n == 1:
                            turn_x(f)
                        if n >= GU0 and n - GU0 < JT:
                            gate_up(f, n - GU0)
                        if n >= DS - 2:
                            down(f, n - DS + 2)

            chunk(0, True, False, False)
            chunk(1, True, True, False)
            with pe.Fori(1, NCH // 2) as p:
                for par in range(2):
                    chunk(p * 2 + par, True, True, True)
            chunk(NCH, False, True, True)
            down(NCH - 1, 2)
            down(NCH - 1, 3)


def kernel(x, ctx_1024, L0_xattn_in_proj_w, L0_xattn_conv_w, L0_xattn_conv_b, L0_xattn_x_proj_w,
           L0_xattn_dt_proj_w, L0_xattn_dt_proj_b, L0_xattn_A_log, L0_xattn_D, L0_ffn_lut,
           L0_ffn_gate_idx, L0_ffn_up_idx, L0_ffn_down_idx):
    import numpy as np
    import concourse.bacc as bacc
    from concourse.bass_utils import run_bass_kernel_spmd

    part = 128

    def tiles(a):
        a = np.asarray(a)
        n = -(-a.shape[0] // part)
        full = np.zeros((n * part, a.shape[1]), a.dtype)
        full[:a.shape[0]] = a
        return full.reshape(n, part, a.shape[1]).transpose(1, 0, 2).reshape(part, -1)

    def lay(a):
        return np.ascontiguousarray(np.asarray(a))

    arrays = {
        "ctx_t": lay(np.asarray(ctx_1024).transpose(0, 2, 1)),
        "x": lay(x),
        "win_t": lay(np.asarray(L0_xattn_in_proj_w).T),
        "conv_w": lay(L0_xattn_conv_w),
        "conv_b": lay(L0_xattn_conv_b),
        "xproj_t": lay(np.asarray(L0_xattn_x_proj_w).T),
        "dt_t": lay(np.asarray(L0_xattn_dt_proj_w).T),
        "dt_b": lay(L0_xattn_dt_proj_b),
        "a_log": lay(L0_xattn_A_log),
        "d_skip": lay(L0_xattn_D),
        "lut": lay(L0_ffn_lut),
        "idx": lay(np.concatenate([tiles(np.asarray(L0_ffn_gate_idx).T), tiles(np.asarray(L0_ffn_up_idx).T),
                                   tiles(np.asarray(L0_ffn_down_idx).T)], axis=1)),
    }
    nc = bacc.Bacc("TRN2", target_bir_lowering=False, num_devices=1)
    args = [nc.dram_tensor(f"in_{k}", a.shape, mybir.dt.from_np(a.dtype), kind="ExternalInput").ap()
            for k, a in arrays.items()]
    out = nc.dram_tensor("out_0", arrays["x"].shape, F32, kind="ExternalOutput").ap()
    mamba_ffn(nc, *args, out)
    r = run_bass_kernel_spmd(nc, [{f"in_{k}": a for k, a in arrays.items()}], core_ids=[0])
    return r.results[0]["out_0"]
```

```python
from contextlib import ExitStack

import concourse.bass as bass
import concourse.mybir as mybir

ALU = mybir.AluOpType
ACT = mybir.ActivationFunctionType
AX = mybir.AxisListType
F32 = mybir.dt.float32
F16 = mybir.dt.float16
I32 = mybir.dt.int32
I16 = mybir.dt.int16

P = 128
EPS = 1e-5


def after(eng, sem, count):
    if isinstance(count, int) and count <= 0:
        return
    eng.wait_ge(sem, count)


def settled(eng, sem):
    eng.sem_inc(sem, 1)


def mamba_ffn(nc, ctx_t, x, win_t, conv_w, conv_b, xproj_t, dt_t, dt_b, a_log, d_skip, lut, idx, out):
    NB, DM, L = ctx_t.shape
    DI = win_t.shape[1]
    DS = a_log.shape[1]
    DR = dt_t.shape[0]
    KC = conv_w.shape[1]
    NX = xproj_t.shape[1]
    NLUT = lut.shape[0]
    HID = x.shape[2]
    F = idx.shape[1]
    INTER = 1376
    KT = HID // P
    ET = DI // P
    KM = DM // P
    LT = L // P
    JT = -(-INTER // P)
    TC = 256
    CT = TC // P
    NCH = NB * L // TC
    UP0 = KT * INTER
    DN0 = 2 * KT * INTER
    PIECES = 8
    PW = F // (NB * PIECES)
    NPAIR = NLUT // 2
    ACT_AFF = [4, 3, 3, 3, 3, 4, 4, 4]
    POOL_AFF = [NPAIR - n for n in ACT_AFF]
    SLOTS = 4
    AHEAD = 2
    GR = 4
    NG = DS // GR
    assert F == NB * PIECES * PW and F == DN0 + JT * HID and L == CT * P * 2
    assert NX == DR + 2 * DS

    def rows(j):
        return min(P, INTER - j * P)

    def proj_bank(b, et):
        return bank[(0, 1, 6, 7)[et] if isinstance(b, int) and b == 0 else et % 2]

    def pairs(b, s, share):
        return b * sum(share) + s // PIECES * sum(share) + sum(share[:s % PIECES])

    def dram(name, shape):
        return nc.dram_tensor(name, shape, F32, kind="Internal").ap()

    dd_d = dram("dd_scratch", [NCH, P, 2, ET, TC])
    b_d = dram("b_scratch", [NCH, DS, TC])
    ct_d = dram("ct_scratch", [NCH, P, CT, DS])
    ud_d = dram("ud_scratch", [NCH, CT, P, DI])
    gz_d = dram("gz_scratch", [NCH, CT, P, L])

    ctx = ExitStack()
    with ctx:
        def sem(name):
            return ctx.enter_context(nc.semaphore(name))

        def sb(name, shape, dt=F32):
            return ctx.enter_context(nc.sbuf_tensor(name, shape, dt))

        bank = [ctx.enter_context(nc.psum_tensor(f"bank{i}", [P, 512], F32)) for i in range(8)]

        w_hi = sb("w_hi", [P, F], F16)
        w_lo = sb("w_lo", [P, F], F16)
        ident = sb("ident", [P, P])
        neg_a = sb("neg_a", [P, ET, DS])
        sc = sb("sc", [P, 8])
        lut_s = sb("lut_s", [P, NLUT])
        lut_d = sb("lut_d", [P, NPAIR])
        half = sb("half", [P, LT])
        out_scale, tanh_scale = sc[:, 0:1], sc[:, 1:2]

        ctxA = ExitStack()

        def sa(name, shape, dt=F32):
            return ctxA.enter_context(nc.sbuf_tensor(name, shape, dt))

        ctx_sb = sa("ctx_sb", [P, KM, L])
        win_sb = sa("win_sb", [P, KM, DI])
        xpad = sa("xpad", [P, ET, L + KC - 1])
        conv_diag = sa("conv_diag", [P, ET, KC, P])
        x_sb = sa("x_sb", [P, LT, HID])
        zn = sa("zn", [P, LT, HID])
        v_tanh = sa("v_tanh", [P, ET, L])
        pair = sa("pair", [P, 2, NPAIR, PW])
        xproj_sb = sa("xproj_sb", [P, ET, NX])
        dt_sb = sa("dt_sb", [DR, DI])
        xdbl_sb = sa("xdbl_sb", [NX, L])
        d_diag = sa("d_diag", [P, ET, P])
        cw_sb = sa("cw_sb", [P, ET, KC])
        vec = sa("vec", [P, 3, ET])
        cb_half = sa("cb_half", [P, ET])
        u_sb = sa("u_sb", [P, ET, L])
        e_exp = sa("e_exp", [P, ET, L])
        e_ln = sa("e_ln", [P, ET, L])
        e_relu = sa("e_relu", [P, ET, L])
        ud_st = sa("ud_st", [P, 2, DI])
        gz_st = sa("gz_st", [P, 2, LT, P])
        ct_st = sa("ct_st", [P, LT, DS])
        stats = sa("stats", [P, LT, 6])
        mv = sa("mv", [P, LT, 2])
        zsc = sa("zsc", [P, 4, LT])
        idx_sb = sa("idx_sb", [P, 2, PW], I32)
        idx16 = sa("idx16", [P, 2, PW], I16)
        bit0 = sa("bit0", [P, 2, PW], I16)
        bits = sa("bits", [P, 3, PW], I16)
        lut_in = sa("lut_in", [P, NLUT])
        lut_i = sa("lut_i", [P, 4], I32)
        ctxA.close()

        ctxB = ctx.enter_context(ExitStack())

        def sB(name, shape, dt=F32):
            return ctxB.enter_context(nc.sbuf_tensor(name, shape, dt))

        dd = sB("dd", [P, 2, 2, ET, TC])
        b_rows = sB("b_rows", [P, 2, GR, TC])
        ct = sB("ct", [P, 2, CT, DS])
        init = sB("init", [P, CT, DI])
        dec = sB("dec", [P, SLOTS, ET, TC])
        db = sB("db", [P, SLOTS, ET, TC])
        h = sB("h", [P, SLOTS, ET, TC])
        h_last = sB("h_last", [P, DS, ET])
        acc = sB("acc", [P, CT, DI])
        gz = sB("gz", [P, CT, DI])
        x_in = sB("x_in", [P, CT, HID])
        x1 = sB("x1", [P, 2, CT, HID])
        xn = sB("xn", [P, CT, HID])
        xt_hi = sB("xt_hi", [P, KT, TC], F16)
        xt_lo = sB("xt_lo", [P, KT, TC], F16)
        g_tanh = sB("g_tanh", [P, 2, TC])
        u_gate = sB("u_gate", [P, 2, 2, TC])
        q_gate = sB("q_gate", [P, 2, 2, TC])
        h_hi = sB("h_hi", [P, JT + 1, TC], F16)
        h_lo = sB("h_lo", [P, JT + 1, TC], F16)
        out_sb = sB("out_sb", [P, CT, HID])
        stats2 = sB("stats2", [P, CT, 6])
        mv2 = sB("mv2", [P, CT, 2])
        nsc = sB("nsc", [P, 4, CT])

        names = """win_loaded params_loaded lut_loaded vec_loaded ctx_loaded xa_loaded ident_zero ident_ready setup
            setup_act half_ready xp_ready xpad_ready pad_zero v_ready vhalf_ready u_ready xdbl_ready
            xdbl_sb_ready ud_ready ud_free dt_ready eabs_ready erelu_ready eexp_ready w_ready t_ready ln_ready
            lnt_ready sp_ready delta_ready ctt_ready ct_ready zstat zsc_ready zpow zn_ready ztanh_ready gz_ready
            gzt_ready gz_st_ready cast_ready bit0_ready masks_ready pairs_act pairs_pool level picked whi_ready
            wlo_ready b_stored ct_stored dd_stored phase_a scan_done exp_done db_done ht_ready stt_done hl_saved
            init_loaded gz_loaded x_loaded x1_ready fin_stat npow xn_ready xnt_ready xhi_ready xlo_ready
            gu_ready us_ready q_ready hs_ready hhi_ready hlo_ready dn_ready out_ready passed_sp
            passed_pool passed_dve passed_pe""".split()
        S = {name: sem(name) for name in names}
        idx_loaded = [sem(f"idx_loaded{i}") for i in range(2)]
        ud_stored = [sem(f"ud_stored{i}") for i in range(2)]
        gz_stored = [sem(f"gz_stored{i}") for i in range(2)]
        dd_loaded = [sem(f"dd_loaded{i}") for i in range(2)]
        b_loaded = [sem(f"b_loaded{i}") for i in range(2)]
        out_stored = [sem(f"out_stored{i}") for i in range(CT)]

        block = ctx.enter_context(nc.Block())

        GU0 = 5
        down_parts = [
            [(0, j) for j in range(5)],
            [(0, j) for j in range(5, 8)] + [(1, 0)],
            [(1, j) for j in range(1, 5)],
            [(1, j) for j in range(5, 8)] + [(0, 8), (0, 9)],
            [(0, 10), (1, 8), (1, 9), (1, 10)],
        ]
        JG = -(-JT // 2)

        @block.sync
        def _(sp):
            sp.dma_start(lut_in[:], lut.rearrange("(a n) -> a n", a=1).partition_broadcast(P)
                         .rearrange("p a n -> p (a n)")).then_inc(S["lut_loaded"], 16)

            def load_ctx(b):
                sp.dma_start(ctx_sb[:], ctx_t[bass.ds(b, 1)].rearrange("a (k p) l -> p (a k) l", p=P))\
                    .then_inc(S["ctx_loaded"], 16)

            def load_x(b):
                sp.dma_start(x_sb[:], x[bass.ds(b, 1)].rearrange("a (s p) h -> p (a s) h", p=P))\
                    .then_inc(S["xa_loaded"], 16)

            def load_idx(b, s):
                sp.dma_start(idx_sb[:, s % 2, :], idx[:, bass.ds(b * (PIECES * PW) + s * PW, PW)])\
                    .then_inc(idx_loaded[s % 2], 16)

            def half_view(d, b, hf):
                return d[bass.ds(b * 2 + hf, 1)]

            def store_ud(b, tts):
                for tt in tts:
                    sp.wait_ge(S["ud_free"], b * LT + tt + 1)
                    settled(sp, S["passed_sp"])
                    sp.dma_start(half_view(ud_d, b, tt // CT)[:, tt % CT].rearrange("a p e -> p (a e)"),
                                 ud_st[:, tt % 2, :]).then_inc(ud_stored[tt % 2], 16)

            def store_gz(b, sts):
                for st in sts:
                    sp.wait_ge(S["gz_st_ready"], b * LT + st + 1)
                    settled(sp, S["passed_sp"])
                    for hf in range(2):
                        sp.dma_start(
                            half_view(gz_d, b, hf)[:, :, :, st * P:(st + 1) * P].rearrange("a c p s -> p (a c) s"),
                            gz_st[:, st % 2, hf * CT:(hf + 1) * CT, :]).then_inc(gz_stored[st % 2], 16)

            def store_dd(b, et):
                sp.wait_ge(S["sp_ready"], b * ET + et + 1)
                settled(sp, S["passed_sp"])
                dst = dd_d[bass.ds(b * 2, 2)]
                for i, src in enumerate((e_relu, e_ln)):
                    sp.dma_start(dst[:, :, i, et, :].rearrange("c p t -> p c t"),
                                 src[:, et, :].rearrange("p (c t) -> p c t", t=TC)).then_inc(S["dd_stored"], 16)

            load_ctx(0)
            sp.dma_start(win_sb[:], win_t.rearrange("(k p) e -> p k e", p=P)).then_inc(S["win_loaded"], 16)
            sp.dma_start(cw_sb[:], conv_w.rearrange("(t p) k -> p t k", p=P)).then_inc(S["vec_loaded"], 16)
            load_idx(0, 0)
            load_idx(0, 1)
            load_x(0)
            sp.dma_start(xproj_sb[:], xproj_t.rearrange("(t p) k -> p t k", p=P)).then_inc(S["params_loaded"], 16)
            sp.dma_start(dt_sb[:], dt_t).then_inc(S["params_loaded"], 16)
            for s in range(2):
                sp.wait_ge(S["cast_ready"], s + 1)
                load_idx(0, s + 2)

            def load_dd(c, par):
                sp.dma_start(dd[:, par], dd_d[bass.ds(c, 1)].rearrange("a p k t l -> p (a k) t l"))\
                    .then_inc(dd_loaded[par], 16)
                sp.dma_start(ct[:, par], ct_d[bass.ds(c, 1)].rearrange("a p c n -> p (a c) n"))\
                    .then_inc(dd_loaded[par], 16)

            def load_b(c, g):
                sp.dma_start(b_rows[:, g % 2],
                             b_d[bass.ds(c, 1), g * GR:(g + 1) * GR, :].partition_broadcast(P)
                             .rearrange("p a n t -> p (a n) t")).then_inc(b_loaded[g % 2], 16)

            def load_init(c):
                sp.dma_start(init[:], ud_d[bass.ds(c, 1)].rearrange("a c p e -> p (a c) e"))\
                    .then_inc(S["init_loaded"], 16)

            def load_end(c):
                sp.dma_start(gz[:], gz_d[bass.ds(c, 1)].rearrange("a c p e -> p (a c) e"))\
                    .then_inc(S["gz_loaded"], 16)
                sp.dma_start(x_in[:], x.rearrange("b (v c p) h -> (b v) p c h", p=P, c=CT)[bass.ds(c, 1)]
                             .rearrange("a p c h -> p (a c) h")).then_inc(S["x_loaded"], 16)

            def batch(b, last=False):
                for s in range(PIECES):
                    if not (last and s + 4 >= PIECES):
                        sp.wait_ge(S["cast_ready"], b * PIECES + s + 3)
                        settled(sp, S["passed_sp"])
                        load_idx(b, s + 4)
                    if s == 0 and not last:
                        sp.wait_ge(S["xp_ready"], b * ET + ET)
                        settled(sp, S["passed_sp"])
                        load_ctx(b + 1)
                    if s == 1:
                        sp.wait_ge(S["xdbl_sb_ready"], b + 1)
                        settled(sp, S["passed_sp"])
                        sp.dma_start(b_d[bass.ds(b * 2, 2)].rearrange("c n t -> n c t"),
                                     xdbl_sb[DR:DR + DS, :].rearrange("n (c t) -> n c t", t=TC))\
                            .then_inc(S["b_stored"], 16)
                    if s == 2:
                        if not last:
                            sp.wait_ge(S["zn_ready"], b * LT + LT)
                            settled(sp, S["passed_sp"])
                            load_x(b + 1)
                        sp.wait_ge(S["ct_ready"], b + 1)
                        settled(sp, S["passed_sp"])
                        for hf in range(2):
                            sp.dma_start(half_view(ct_d, b, hf).rearrange("a p c n -> p (a c) n"),
                                         ct_st[:, hf * CT:(hf + 1) * CT, :]).then_inc(S["ct_stored"], 16)
                    if s == 3 and last:
                        sp.wait_ge(S["dd_stored"], b * (ET * 32))
                        for i in range(2):
                            sp.wait_ge(ud_stored[i], b * (LT * 8))
                        sp.wait_ge(S["b_stored"], NB * 16)
                        sp.wait_ge(S["ct_stored"], NB * 32)
                        sp.wait_ge(S["v_ready"], NB * ET)
                        sp.wait_ge(S["zn_ready"], NB * LT)
                        load_dd(0, 0)
                        load_b(0, 0)
                        load_b(0, 1)
                        load_init(0)
                    if s == 4:
                        store_ud(b, (0, 1))
                    if s == 5:
                        store_ud(b, (2, 3))
                        store_dd(b, 0)
                    if s == 6:
                        store_gz(b, (0, 1))
                        store_dd(b, 1)
                    if s == 7:
                        store_gz(b, (2, 3))
                        store_dd(b, 2)
                        store_dd(b, 3)

            batch(0)
            with sp.Fori(1, NB - 1) as b:
                batch(b)
            batch(NB - 1, last=True)

            for i in range(2):
                sp.wait_ge(ud_stored[i], NB * LT * 8)
                sp.wait_ge(gz_stored[i], NB * LT * 16)
            sp.wait_ge(S["dd_stored"], NB * ET * 32)
            sp.wait_ge(S["b_stored"], NB * 16)
            sp.wait_ge(S["ct_stored"], NB * 32)
            sp.wait_ge(S["phase_a"], 4)

            load_end(0)

            def store(f):
                for tt in range(CT):
                    sp.wait_ge(S["out_ready"], CT + f * CT + tt + 1)
                    settled(sp, S["passed_sp"])
                    sp.dma_start(out.rearrange("b (v c p) h -> (b v c) p h", p=P, c=CT)[bass.ds(f * CT + tt, 1)]
                                 .rearrange("a p h -> p (a h)"), out_sb[:, tt, :]).then_inc(out_stored[tt], 16)

            def chunk(c, par, more=True, end=True, fin=True):
                if more:
                    after(sp, S["exp_done"], c * DS * ET)
                    settled(sp, S["passed_sp"])
                    after(sp, S["db_done"], c * DS)
                    settled(sp, S["passed_sp"])
                    after(sp, S["stt_done"], c * DS * CT)
                    settled(sp, S["passed_sp"])
                    load_dd(c + 1, 1 - par)
                for g in range(2, NG):
                    sp.wait_ge(S["db_done"], c * DS + (g - 1) * GR)
                    settled(sp, S["passed_sp"])
                    load_b(c, g)
                    if g == 2 and end:
                        sp.wait_ge(S["x1_ready"], c * 2)
                        settled(sp, S["passed_sp"])
                        load_end(c)
                    if g == 2 and more:
                        sp.wait_ge(S["stt_done"], c * DS * CT + CT)
                        settled(sp, S["passed_sp"])
                        load_init(c + 1)
                if fin:
                    store(c - 2)
                if more:
                    for g in range(2):
                        sp.wait_ge(S["db_done"], c * DS + (g + NG - 1) * GR)
                        settled(sp, S["passed_sp"])
                        load_b(c + 1, g)

            chunk(0, 0, end=False, fin=False)
            chunk(1, 1, fin=False)
            with sp.Fori(1, NCH // 2 - 1) as p:
                for par in range(2):
                    chunk(p * 2 + par, par)
            chunk(NCH - 2, 0)
            chunk(NCH - 1, 1, more=False)
            store(NCH - 2)
            store(NCH - 1)
            for tt in range(CT):
                sp.wait_ge(out_stored[tt], 16 + NCH * 16)

        @block.gpsimd
        def _(pool):
            pool.memset(ident[:], 0.0).then_inc(S["ident_zero"], 1)
            pool.memset(half[:], -0.5).then_inc(S["half_ready"], 1)
            for i in range(ET):
                pool.memset(xpad[:, i, 0:KC - 1], 0.0).then_inc(S["pad_zero"], 1)
            pool.wait_ge(S["ident_zero"], 1)
            pool.affine_select(out=ident[:], in_=ident[:], compare_op=ALU.not_equal, fill=1.0, base=0,
                               pattern=[[-1, P]], channel_multiplier=1).then_inc(S["ident_ready"], 1)
            pool.wait_ge(S["half_ready"], 1)
            pool.wait_ge(S["setup"], 1)

            def piece(b, s):
                pool.wait_ge(S["bit0_ready"], b * PIECES + s + 1)
                after(pool, S["level"], b * PIECES + s - 1)
                for j in range(ACT_AFF[s % PIECES], NPAIR):
                    settled(pool, S["passed_pool"])
                    pool.tensor_scalar(pair[:, s % 2, j, :], bit0[:, s % 2, :], lut_d[:, j:j + 1],
                                       lut_s[:, 2 * j:2 * j + 1], ALU.mult, ALU.add).then_inc(S["pairs_pool"], 1)

            def low_part(b, s):
                pool.wait_ge(S["whi_ready"], b * PIECES + s + 1)
                cols = bass.ds(b * (PIECES * PW) + s * PW, PW)
                pool.tensor_tensor(w_lo[:, cols], pair[:, s % 2, 0, :], w_hi[:, cols], ALU.subtract)\
                    .then_inc(S["wlo_ready"], 1)

            def z_scales(b):
                pool.wait_ge(S["zstat"], b * 6 + 6)
                after(pool, S["zn_ready"], b * LT)
                pool.tensor_tensor(zsc[:, 2, :], zsc[:, 0, :], half[:], ALU.pow).then_inc(S["zpow"], 1)
                pool.wait_ge(S["zpow"], b * 2 + 1)
                settled(pool, S["passed_pool"])
                pool.tensor_scalar(zsc[:, 3, :], zsc[:, 2, :], 0.5, 1.0, ALU.mult, ALU.mult)\
                    .then_inc(S["zpow"], 1)

            def z_half(b):
                pool.wait_ge(S["zpow"], b * 2 + 2)
                after(pool, S["gzt_ready"], b * LT)
                for st in range(LT):
                    settled(pool, S["passed_pool"])
                    pool.tensor_scalar(zn[:, st, :], x_sb[:, st, :], zsc[:, 1, st:st + 1], zsc[:, 3, st:st + 1],
                                       ALU.add, ALU.mult).then_inc(S["zn_ready"], 1)

            def delta(b, et):
                pool.wait_ge(S["lnt_ready"], b * ET + et + 1)
                pool.tensor_tensor(e_relu[:, et, :], e_ln[:, et, :], e_relu[:, et, :], ALU.add)\
                    .then_inc(S["delta_ready"], 1)
                pool.wait_ge(S["delta_ready"], b * ET + et + 1)
                pool.tensor_tensor(e_ln[:, et, :], e_relu[:, et, :], u_sb[:, et, :], ALU.mult)\
                    .then_inc(S["sp_ready"], 1)

            def batch(b, last=False, late=0):
                for s in range(PIECES):
                    if s or not isinstance(b, int) or b:
                        low_part(b, s - 1)
                    if not (last and s == PIECES - 1):
                        piece(b, s + 1)
                    if s == 0:
                        z_scales(b)
                    if s == 1:
                        z_half(b)
                    if s >= 4 + late:
                        delta(b, s - 4 - late)
                    if s == PIECES - 1 and late:
                        delta(b, ET - 1)

            piece(0, 0)
            batch(0, late=1)
            with pool.Fori(1, NB - 1) as b:
                batch(b)
            batch(NB - 1, last=True)
            low_part(NB - 1, PIECES - 1)

            pool.wait_ge(S["wlo_ready"], NB * PIECES)
            pool.sem_inc(S["phase_a"], 1)
            pool.wait_ge(S["phase_a"], 4)

            def state(c, par, n):
                if n == 0:
                    pool.wait_ge(dd_loaded[par], c * 16 + (32 if par == 0 else 16))
                if n % GR == 0:
                    g = n // GR
                    pool.wait_ge(b_loaded[g % 2], c * (NG // 2 * 16) + 16 * (g // 2 + 1))
                after(pool, S["scan_done"], c * (DS * ET) + (n - SLOTS + 1) * ET)
                pool.tensor_tensor(
                    db[:, n % SLOTS], dd[:, par, 1],
                    b_rows[:, (n // GR) % 2, n % GR:n % GR + 1, :].to_broadcast([P, ET, TC]),
                    ALU.mult).then_inc(S["db_done"], 1)

            def normal(f):
                pool.wait_ge(S["fin_stat"], f * 4 + 4)
                after(pool, S["xn_ready"], f * CT)
                pool.tensor_tensor(nsc[:, 2, :], nsc[:, 0, :], half[:, 0:CT], ALU.pow).then_inc(S["npow"], 1)
                pool.wait_ge(S["npow"], f * 2 + 1)
                settled(pool, S["passed_pool"])
                pool.tensor_scalar(nsc[:, 3, :], nsc[:, 2, :], 256.0, 1.0, ALU.mult, ALU.mult)\
                    .then_inc(S["npow"], 1)
                pool.wait_ge(S["npow"], f * 2 + 2)
                after(pool, S["xnt_ready"], f * 2)

            def normal_rows(f, par):
                for tt in range(CT):
                    settled(pool, S["passed_pool"])
                    pool.tensor_scalar(xn[:, tt, :], x1[:, par, tt, :], nsc[:, 1, tt:tt + 1], nsc[:, 3, tt:tt + 1],
                                       ALU.add, ALU.mult).then_inc(S["xn_ready"], 1)

            def gated(f, g):
                two = 2 if g < JT // 2 else 1
                rp = rows(2 * g)
                slot = g % 2
                pool.wait_ge(S["q_ready"], f * JT + 2 * g + two)
                pool.wait_ge(S["us_ready"], f * JT + 2 * g + two)
                pool.tensor_tensor(u_gate[0:rp, slot, 0:two, :], q_gate[0:rp, slot, 0:two, :],
                                   u_gate[0:rp, slot, 0:two, :], ALU.mult).then_inc(S["hs_ready"], 1)

            def gated_low(f, g):
                two = 2 if g < JT // 2 else 1
                rp = rows(2 * g)
                slot = g % 2
                pool.wait_ge(S["hhi_ready"], f * 6 + g + 1)
                if g == 0:
                    after(pool, S["dn_ready"], f * CT)
                pool.tensor_tensor(h_lo[0:rp, 2 * g:2 * g + two, :], u_gate[0:rp, slot, 0:two, :],
                                   h_hi[0:rp, 2 * g:2 * g + two, :], ALU.subtract).then_inc(S["hlo_ready"], 1)

            def ffn(f, par, m):
                if m == 1:
                    normal(f)
                    normal_rows(f, par)
                if m >= 8 and m % 2 == 0 and m <= DS:
                    gated(f, (m - 8) // 2)
                    if m == DS:
                        gated(f, JG - 1)
                if m >= 9 and m % 2 == 1 and m <= DS + 1:
                    gated_low(f, (m - 9) // 2)
                    if m == DS + 1:
                        gated_low(f, JG - 1)

            def chunk(c, par, ssm=True, more=True, prev=True, rest=True):
                for n in range(DS):
                    if ssm and n + AHEAD < DS:
                        state(c, par, n + AHEAD)
                    if more and n + AHEAD >= DS:
                        state(c + 1, 1 - par, n + AHEAD - DS)
                    if rest:
                        ffn(c - 2, par, DS + n)
                    if prev:
                        ffn(c - 1, 1 - par, n)

            for n in range(AHEAD):
                state(0, 0, n)
            chunk(0, 0, prev=False, rest=False)
            chunk(1, 1, rest=False)
            with pool.Fori(1, NCH // 2 - 1) as p:
                for par in range(2):
                    chunk(p * 2 + par, par)
            chunk(NCH - 2, 0)
            chunk(NCH - 1, 1, more=False)
            chunk(NCH, 0, ssm=False, more=False)
            chunk(NCH + 1, 1, ssm=False, more=False, prev=False)

        @block.scalar
        def _(act):
            with nc.allow_non_contiguous_dma(reason="512 numbers each"):
                for i, v in enumerate((conv_b, dt_b, d_skip)):
                    act.dma_start(vec[:, i, :], v.rearrange("(t p) -> p t", p=P)).then_inc(S["vec_loaded"], 16)
            act.dma_start(neg_a[:], a_log.rearrange("(t p) n -> p t n", p=P)).then_inc(S["vec_loaded"], 16)
            act.wait_ge(S["vec_loaded"], 80)
            act.activation(neg_a[:], neg_a[:], ACT.Exp).then_inc(S["setup_act"], 1)
            act.mul(cb_half[:], vec[:, 0, :], 0.5).then_inc(S["setup_act"], 1)
            act.wait_ge(S["setup_act"], 2)
            act.mul(neg_a[:], neg_a[:], -1.0).then_inc(S["setup_act"], 1)
            act.wait_ge(S["pad_zero"], ET)

            def piece(b, s):
                act.wait_ge(S["bit0_ready"], b * PIECES + s + 1)
                after(act, S["level"], b * PIECES + s - 1)
                for j in reversed(range(ACT_AFF[s % PIECES])):
                    if j == 0:
                        after(act, S["wlo_ready"], b * PIECES + s - 1)
                    act.activation(pair[:, s % 2, j, :], bit0[:, s % 2, :], ACT.Identity, scale=lut_d[:, j:j + 1],
                                   bias=lut_s[:, 2 * j:2 * j + 1]).then_inc(S["pairs_act"], 1)

            def narrow(b, s):
                act.wait_ge(idx_loaded[s % 2], b * (PIECES * 8) + 16 * (s // 2) + 16)
                after(act, S["masks_ready"], b * (3 * PIECES) + 3 * (s - 1))
                act.copy(idx16[:, s % 2, :], idx_sb[:, s % 2, :]).then_inc(S["cast_ready"], 1)

            def high_part(b, s):
                act.wait_ge(S["level"], b * PIECES + s + 1)
                act.copy(w_hi[:, bass.ds(b * (PIECES * PW) + s * PW, PW)], pair[:, s % 2, 0, :])\
                    .then_inc(S["whi_ready"], 1)

            def pad(b, et):
                act.wait_ge(S["xp_ready"], b * ET + et + 1)
                after(act, S["v_ready"], b * ET)
                act.copy(xpad[:, et, KC - 1:], proj_bank(b, et)[:]).then_inc(S["xpad_ready"], 1)

            def gate_u(b, et):
                act.wait_ge(S["v_ready"], b * ET + et + 1)
                after(act, S["lnt_ready"], b * ET)
                after(act, S["gz_ready"], b * LT)
                act.activation(e_exp[:, et, :], bank[2 + et][:], ACT.Identity, scale=0.5,
                               bias=cb_half[:, et:et + 1]).then_inc(S["vhalf_ready"], 1)
                act.activation(v_tanh[:, et, :], bank[2 + et][:], ACT.Tanh, scale=0.5,
                               bias=cb_half[:, et:et + 1]).then_inc(S["vhalf_ready"], 1)

            def z_tanh(b, st):
                act.wait_ge(S["zn_ready"], b * LT + st + 1)
                act.wait_ge(S["u_ready"], b * ET + ET)
                act.activation(v_tanh[:, st, :], zn[:, st, :], ACT.Tanh).then_inc(S["ztanh_ready"], 1)

            def low_rank(b):
                act.wait_ge(S["xdbl_ready"], b + 1)
                after(act, S["b_stored"], b * 16)
                after(act, S["ctt_ready"], b)
                act.copy(xdbl_sb[:], bank[4][0:NX, :]).then_inc(S["xdbl_sb_ready"], 1)

            def soft(b, et):
                act.wait_ge(S["dt_ready"], b * ET + et + 1)
                if et == 0:
                    after(act, S["dd_stored"], b * (ET * 32))
                act.activation(e_exp[:, et, :], bank[et % 2][:], ACT.Abs, bias=vec[:, 1, et:et + 1])\
                    .then_inc(S["eabs_ready"], 1)
                act.activation(e_relu[:, et, :], bank[et % 2][:], ACT.Relu, bias=vec[:, 1, et:et + 1])\
                    .then_inc(S["erelu_ready"], 1)
                act.wait_ge(S["eabs_ready"], b * ET + et + 1)
                act.activation(e_exp[:, et, :], e_exp[:, et, :], ACT.Exp, scale=-1.0)\
                    .then_inc(S["eexp_ready"], 1)

            def log(b, et):
                act.wait_ge(S["t_ready"], b * ET + et + 1)
                act.activation(e_ln[:, et, :], e_ln[:, et, :], ACT.Ln).then_inc(S["ln_ready"], 1)

            def c_rows(b):
                act.wait_ge(S["ctt_ready"], b + 1)
                after(act, S["ct_stored"], b * 32)
                act.copy(ct_st[:], bank[5][:, 0:LT * NX].rearrange("p (t k) -> p t k", k=NX)[:, :, DR + DS:NX])\
                    .then_inc(S["ct_ready"], 1)

            def ud_out(b, tt):
                act.wait_ge(S["ud_ready"], b * LT + tt + 1)
                after(act, ud_stored[tt % 2], b * 32 + 16 * (tt // 2))
                act.copy(ud_st[:, tt % 2, :], bank[6 + tt % 2][:]).then_inc(S["ud_free"], 1)

            def gz_out(b, st):
                act.wait_ge(S["gzt_ready"], b * LT + st + 1)
                after(act, gz_stored[st % 2], b * 64 + 32 * (st // 2))
                act.copy(gz_st[:, st % 2], bank[6 + st % 2][:].rearrange("p (l s) -> p l s", s=P))\
                    .then_inc(S["gz_st_ready"], 1)

            def batch(b, last=False, late=0):
                gates = (0, 1, 1, 2) if late else (None, None, None, 0)
                for s in range(PIECES):
                    if s or not late:
                        high_part(b, s - 1)
                    if not (last and s == PIECES - 1):
                        piece(b, s + 1)
                    if not (last and s + 2 >= PIECES):
                        narrow(b, s + 2)
                    for et in range(ET):
                        if s == gates[et]:
                            gate_u(b, et)
                    if s == 1 + late:
                        low_rank(b)
                    if s in (1 + late, 2 + late):
                        soft(b, 2 * (s - late) - 2)
                        soft(b, 2 * (s - late) - 1)
                    if s == 2 + late:
                        c_rows(b)
                    if s == 3 + late:
                        for et in range(ET):
                            log(b, et)
                    if s == 4:
                        ud_out(b, 0)
                        ud_out(b, 1)
                        z_tanh(b, 0)
                        z_tanh(b, 1)
                    if s == 5:
                        ud_out(b, 2)
                        ud_out(b, 3)
                        if not last:
                            pad(b + 1, 0)
                            pad(b + 1, 1)
                        z_tanh(b, 2)
                        z_tanh(b, 3)
                    if s == 6:
                        if not last:
                            pad(b + 1, 2)
                            pad(b + 1, 3)
                        gz_out(b, 0)
                        gz_out(b, 1)
                    if s == 7:
                        gz_out(b, 2)
                        gz_out(b, 3)
                    if s == 7 and not last:
                        gate_u(b + 1, 0)
                        gate_u(b + 1, 1)
                        gate_u(b + 1, 2)

            narrow(0, 0)
            act.wait_ge(S["setup"], 1)
            act.wait_ge(S["setup_act"], 3)
            piece(0, 0)
            narrow(0, 1)
            for et in range(ET):
                pad(0, et)
            batch(0, late=1)
            with act.Fori(1, NB - 1) as b:
                batch(b)
            batch(NB - 1, last=True)
            high_part(NB - 1, PIECES - 1)

            act.wait_ge(S["whi_ready"], NB * PIECES)
            act.sem_inc(S["phase_a"], 1)
            act.wait_ge(S["phase_a"], 4)

            def decay(c, par, n):
                if n == 0:
                    act.wait_ge(dd_loaded[par], c * 16 + (32 if par == 0 else 16))
                for et in range(ET):
                    if et == 0:
                        after(act, S["scan_done"], c * (DS * ET) + (n - SLOTS + 1) * ET)
                    act.activation(dec[:, n % SLOTS, et, :], dd[:, par, 0, et, :], ACT.Exp,
                                   scale=neg_a[:, et, n:n + 1]).then_inc(S["exp_done"], 1)

            def high_x(f):
                for k in range(2):
                    act.wait_ge(S["xnt_ready"], f * 2 + k + 1)
                    if k == 0:
                        after(act, S["gu_ready"], f * JT)
                    act.copy(xt_hi[:, 2 * k:2 * k + 2, :], bank[4 + k][:].rearrange("p (a t) -> p a t", t=TC))\
                        .then_inc(S["xhi_ready"], 1)

            def gate(f, j):
                r = rows(j)
                act.wait_ge(S["gu_ready"], f * JT + j + 1)
                after(act, S["q_ready"], f * JT + j - 1)
                act.activation(g_tanh[0:r, j % 2, :], bank[4 + j % 2][0:r, 0:TC], ACT.Tanh,
                               scale=tanh_scale[0:r, :])
                if j % 2 == 0:
                    after(act, S["hlo_ready"], f * 6 + max(j // 2 - 1, 0))
                act.activation(u_gate[0:r, (j // 2) % 2, j % 2, :], bank[4 + j % 2][0:r, TC:2 * TC], ACT.Identity,
                               scale=2.0 ** -42).then_inc(S["us_ready"], 1)

            def high_h(f, g):
                two = 2 if g < JT // 2 else 1
                rp = rows(2 * g)
                act.wait_ge(S["hs_ready"], f * 6 + g + 1)
                if g == 0:
                    after(act, S["dn_ready"], f * CT)
                act.copy(h_hi[0:rp, 2 * g:2 * g + two, :], u_gate[0:rp, g % 2, 0:two, :])\
                    .then_inc(S["hhi_ready"], 1)

            def ffn(f, m):
                if m == 3:
                    high_x(f)
                if m > GU0 and m - GU0 - 1 < JT:
                    gate(f, m - GU0 - 1)
                if m >= 8 and m % 2 == 0 and m <= DS:
                    high_h(f, (m - 8) // 2)
                    if m == DS:
                        high_h(f, JG - 1)

            def chunk(c, par, ssm=True, more=True, prev=True, rest=True):
                for n in range(DS):
                    if ssm and n + AHEAD < DS:
                        decay(c, par, n + AHEAD)
                    if more and n + AHEAD >= DS:
                        decay(c + 1, 1 - par, n + AHEAD - DS)
                    if rest:
                        ffn(c - 2, DS + n)
                    if prev:
                        ffn(c - 1, n)

            for n in range(AHEAD):
                decay(0, 0, n)
            chunk(0, 0, prev=False, rest=False)
            chunk(1, 1, rest=False)
            with act.Fori(1, NCH // 2 - 1) as p:
                for par in range(2):
                    chunk(p * 2 + par, par)
            chunk(NCH - 2, 0)
            chunk(NCH - 1, 1, more=False)
            chunk(NCH, 0, ssm=False, more=False)
            chunk(NCH + 1, 1, ssm=False, more=False, prev=False)

        @block.vector
        def _(dve):
            step = S["picked"]
            dve.wait_ge(S["lut_loaded"], 16)
            dve.tensor_reduce(sc[:, 2:3], lut_in[:], AX.X, ALU.max, apply_absolute_value=True).then_inc(step, 1)
            dve.wait_ge(step, 1)
            dve.tensor_scalar(sc[:, 3:4], sc[:, 2:3], 1e-12, None, ALU.max).then_inc(step, 1)
            dve.wait_ge(step, 2)
            dve.tensor_scalar(lut_i[:, 0:1], sc[:, 3:4].bitcast(I32), 0x7F800000, None, ALU.bitwise_and)\
                .then_inc(step, 1)
            dve.wait_ge(step, 3)
            dve.tensor_scalar(lut_i[:, 1:2], lut_i[:, 0:1], -1.0, float(0x7F000000), ALU.mult, ALU.add)\
                .then_inc(step, 1)
            dve.wait_ge(step, 4)
            dve.tensor_scalar(lut_s[:], lut_in[:], lut_i[:, 1:2].bitcast(F32), 2.0 ** 10, ALU.mult, ALU.mult)\
                .then_inc(step, 1)
            dve.tensor_scalar(tanh_scale, lut_i[:, 0:1].bitcast(F32), 2.0 ** -19, None, ALU.mult)\
                .then_inc(step, 1)
            dve.tensor_scalar(sc[:, 4:5], lut_i[:, 0:1].bitcast(F32), lut_i[:, 0:1].bitcast(F32), None, ALU.mult)\
                .then_inc(step, 1)
            dve.wait_ge(step, 7)
            dve.tensor_scalar(out_scale, sc[:, 4:5], lut_i[:, 0:1].bitcast(F32), 2.0 ** -5, ALU.mult, ALU.mult)\
                .then_inc(step, 1)
            twos = lut_s[:].rearrange("p (j two) -> p j two", two=2)
            dve.tensor_tensor(lut_d[:], twos[:, :, 1], twos[:, :, 0], ALU.subtract).then_inc(step, 1)
            dve.wait_ge(step, 9)
            dve.sem_inc(S["setup"], 1)
            dve.wait_ge(S["cast_ready"], 1)
            dve.tensor_scalar(bit0[:, 0, :], idx16[:, 0, :], 1, None, ALU.bitwise_and).then_inc(S["bit0_ready"], 1)
            for i in range(2):
                dve.tensor_scalar(bits[:, i, :], idx16[:, 0, :], 2 << i, None, ALU.bitwise_and)\
                    .then_inc(S["masks_ready"], 1)
            dve.wait_ge(S["vec_loaded"], 80)
            dve.wait_ge(S["ident_ready"], 1)
            for et in range(ET):
                for k in range(KC):
                    dve.tensor_scalar(conv_diag[:, et, k, :], ident[:], cw_sb[:, et, k:k + 1], None, ALU.mult)\
                        .then_inc(S["setup"], 1)
                dve.tensor_scalar(d_diag[:, et, :], ident[:], vec[:, 2, et:et + 1], None, ALU.mult)\
                    .then_inc(S["setup"], 1)

            def lowest_bit(b, s):
                dve.wait_ge(S["cast_ready"], b * PIECES + s + 1)
                after(dve, S["pairs_act"], pairs(b, s - 1, ACT_AFF))
                after(dve, S["pairs_pool"], pairs(b, s - 1, POOL_AFF))
                dve.tensor_scalar(bit0[:, s % 2, :], idx16[:, s % 2, :], 1, None, ALU.bitwise_and)\
                    .then_inc(S["bit0_ready"], 1)

            def mask(b, s, i):
                if i == 2:
                    after(dve, S["level"], b * PIECES + s)
                else:
                    after(dve, S["picked"], b * (2 * PIECES) + (9 + 2 * s + i - 1))
                dve.tensor_scalar(bits[:, i, :], idx16[:, s % 2, :], 2 << i, None, ALU.bitwise_and)\
                    .then_inc(S["masks_ready"], 1)

            def select(b, s, more):
                dve.wait_ge(S["pairs_act"], pairs(b, s + 1, ACT_AFF))
                dve.wait_ge(S["pairs_pool"], pairs(b, s + 1, POOL_AFF))
                for i, inc in ((0, S["picked"]), (1, S["picked"]), (2, S["level"])):
                    k = NPAIR >> (i + 1)
                    dst = pair[:, s % 2].rearrange("p (k two r) w -> p k two r w", two=2, r=1 << i)
                    if i:
                        dve.wait_ge(S["picked"], b * (2 * PIECES) + (9 + 2 * s + i))
                    dve.wait_ge(S["masks_ready"], b * (3 * PIECES) + 3 * s + 1 + i)
                    settled(dve, S["passed_dve"])
                    dve.copy_predicated(dst[:, :, 0, 0, :], bits[:, i:i + 1, :].to_broadcast([P, k, PW]),
                                        dst[:, :, 1, 0, :]).then_inc(inc, 1)
                    if i == 0:
                        mask(b, s, 2)
                    elif more:
                        mask(b, s + 1, i - 1)

            def z_stats(b):
                dve.wait_ge(S["xa_loaded"], b * 16 + 16)
                for st in range(LT):
                    dve.bn_stats(stats[:, st, :], x_sb[:, st, :]).then_inc(S["zstat"], 1)
                dve.wait_ge(S["zstat"], b * 6 + 4)
                settled(dve, S["passed_dve"])
                for st in range(LT):
                    m = dve.bn_aggr(mv[:, st, :], stats[:, st, :])
                m.then_inc(S["zsc_ready"], 1)
                dve.wait_ge(S["zsc_ready"], b + 1)
                after(dve, S["zn_ready"], b * LT)
                dve.tensor_scalar(zsc[:, 0, :], mv[:, :, 1], EPS, None, ALU.add).then_inc(S["zstat"], 1)
                dve.tensor_scalar(zsc[:, 1, :], mv[:, :, 0], -1.0, None, ALU.mult).then_inc(S["zstat"], 1)

            def silu_u(b, et):
                dve.wait_ge(S["vhalf_ready"], b * (2 * ET) + 2 * et + 2)
                if et == 0:
                    after(dve, S["sp_ready"], b * ET)
                    after(dve, S["ud_ready"], b * LT)
                dve.scalar_tensor_tensor(u_sb[:, et, :], v_tanh[:, et, :], 1.0, e_exp[:, et, :],
                                         ALU.add, ALU.mult).then_inc(S["u_ready"], 1)

            def silu_z(b, st):
                dve.wait_ge(S["ztanh_ready"], b * LT + st + 1)
                dve.scalar_tensor_tensor(zn[:, st, :], v_tanh[:, st, :], 1.0, zn[:, st, :],
                                         ALU.add, ALU.mult).then_inc(S["gz_ready"], 1)

            def lost(b, et):
                dve.wait_ge(S["eexp_ready"], b * ET + et + 1)
                if et == 0:
                    after(dve, S["dd_stored"], b * (ET * 32))
                dve.tensor_scalar(e_ln[:, et, :], e_exp[:, et, :], 1.0, None, ALU.add).then_inc(S["w_ready"], 1)
                dve.wait_ge(S["w_ready"], b * ET + et + 1)
                dve.scalar_tensor_tensor(e_exp[:, et, :], e_ln[:, et, :], 1.0, e_exp[:, et, :],
                                         ALU.subtract, ALU.subtract).then_inc(S["t_ready"], 1)

            def less_lost(b, et):
                dve.wait_ge(S["ln_ready"], b * ET + et + 1)
                dve.tensor_tensor(e_ln[:, et, :], e_ln[:, et, :], e_exp[:, et, :], ALU.subtract)\
                    .then_inc(S["lnt_ready"], 1)

            def batch(b, last=False, late=0):
                for s in range(PIECES):
                    more = not (last and s == PIECES - 1)
                    if more:
                        lowest_bit(b, s + 1)
                    if s == 0 and not late:
                        silu_u(b, 0)
                    select(b, s, more)
                    if s == 0 and not late:
                        for et in range(1, ET):
                            silu_u(b, et)
                    if s == 1 and late:
                        for et in range(ET - 1):
                            silu_u(b, et)
                    if s == 2 and late:
                        silu_u(b, ET - 1)
                    if s in (2 + late, 3 + late):
                        lost(b, 2 * (s - late) - 4)
                        lost(b, 2 * (s - late) - 3)
                    if s == 4 + late:
                        for et in range(ET):
                            less_lost(b, et)
                    if s in (5, 6):
                        silu_z(b, 2 * s - 10)
                        silu_z(b, 2 * s - 9)
                    if s == 7 and not last:
                        z_stats(b + 1)

            z_stats(0)
            batch(0, late=1)
            with dve.Fori(1, NB - 1) as b:
                batch(b)
            batch(NB - 1, last=True)

            dve.wait_ge(S["level"], NB * PIECES)
            dve.wait_ge(S["setup"], 1 + ET * (KC + 1))
            dve.sem_inc(S["phase_a"], 1)
            dve.wait_ge(S["phase_a"], 4)

            for tt in range(CT):
                dve.sem_inc(S["out_ready"], 1)
                dve.sem_inc(out_stored[tt], 16)

            def scans(c, par, n):
                dve.wait_ge(S["db_done"], c * DS + n + 1)
                after(dve, S["ht_ready"], c * (DS * CT) + (n - SLOTS + 1) * CT)
                if par == 0:
                    after(dve, S["hl_saved"], c * (DS // 2) + max(n - SLOTS + 1, 0))
                elif n < 2:
                    dve.wait_ge(S["hl_saved"], c * (DS // 2) + (DS // 2 - 1) + n)
                dve.wait_ge(S["exp_done"], c * (DS * ET) + (n + 1) * ET)
                for et in range(ET):
                    first = 0.0 if par == 0 else h_last[:, n, et:et + 1]
                    dve.tensor_tensor_scan(h[:, n % SLOTS, et, :], dec[:, n % SLOTS, et, :], db[:, n % SLOTS, et, :],
                                           first, ALU.mult, ALU.add).then_inc(S["scan_done"], 1)

            def outputs(c, par, n):
                for tt in range(CT):
                    dve.wait_ge(S["ht_ready"], c * (DS * CT) + n * CT + tt + 1)
                    if n == 0:
                        if tt == 0:
                            dve.wait_ge(S["init_loaded"], c * 16 + 16)
                            after(dve, S["x1_ready"], c * 2)
                        base = init
                    else:
                        dve.wait_ge(S["stt_done"], c * (DS * CT) + (n - 1) * CT + tt + 1)
                        base = acc
                    dve.scalar_tensor_tensor(acc[:, tt, :], bank[2 * (n % 2) + tt][:], ct[:, par, tt, n:n + 1],
                                             base[:, tt, :], ALU.mult, ALU.add).then_inc(S["stt_done"], 1)

            def save(c, n):
                dve.wait_ge(S["scan_done"], c * (DS * ET) + (n + 1) * ET)
                dve.tensor_copy(h_last[:, n, :], h[:, n % SLOTS, :, TC - 1]).then_inc(S["hl_saved"], 1)

            def finish(c, par):
                dve.wait_ge(S["stt_done"], (c + 1) * (DS * CT))
                dve.wait_ge(S["gz_loaded"], c * 16 + 16)
                dve.tensor_tensor(x1[:, par], acc[:], gz[:], ALU.mult).then_inc(S["x1_ready"], 1)
                dve.wait_ge(S["x_loaded"], c * 16 + 16)
                dve.wait_ge(S["x1_ready"], c * 2 + 1)
                dve.tensor_tensor(x1[:, par], x1[:, par], x_in[:], ALU.add).then_inc(S["x1_ready"], 1)
                dve.wait_ge(S["x1_ready"], c * 2 + 2)
                for tt in range(CT):
                    m = dve.bn_stats(stats2[:, tt, :], x1[:, par, tt, :])
                m.then_inc(S["fin_stat"], 1)
                dve.wait_ge(S["fin_stat"], c * 4 + 1)
                settled(dve, S["passed_dve"])
                for tt in range(CT):
                    m = dve.bn_aggr(mv2[:, tt, :], stats2[:, tt, :])
                m.then_inc(S["fin_stat"], 1)
                dve.wait_ge(S["fin_stat"], c * 4 + 2)
                after(dve, S["xn_ready"], c * CT)
                dve.tensor_scalar(nsc[:, 0, :], mv2[:, :, 1], EPS, None, ALU.add).then_inc(S["fin_stat"], 1)
                dve.tensor_scalar(nsc[:, 1, :], mv2[:, :, 0], -1.0, None, ALU.mult).then_inc(S["fin_stat"], 1)

            def low_x(f):
                for k in range(2):
                    dve.wait_ge(S["xhi_ready"], f * 2 + k + 1)
                    if k == 0:
                        after(dve, S["gu_ready"], f * JT)
                    dve.tensor_tensor(xt_lo[:, 2 * k:2 * k + 2, :], bank[4 + k][:].rearrange("p (a t) -> p a t", t=TC),
                                      xt_hi[:, 2 * k:2 * k + 2, :], ALU.subtract).then_inc(S["xlo_ready"], 1)

            def gate(f, j):
                r = rows(j)
                dve.wait_ge(S["us_ready"], f * JT + j + 1)
                if j % 2 == 0:
                    after(dve, S["hs_ready"], f * 6 + max(j // 2 - 1, 0))
                dve.scalar_tensor_tensor(q_gate[0:r, (j // 2) % 2, j % 2, :], g_tanh[0:r, j % 2, :], 1.0,
                                         bank[4 + j % 2][0:r, 0:TC], ALU.add, ALU.mult).then_inc(S["q_ready"], 1)

            def result(f, par, tt):
                dve.wait_ge(S["dn_ready"], f * CT + tt + 1)
                dve.wait_ge(out_stored[tt], 16 + f * 16)
                dve.scalar_tensor_tensor(out_sb[:, tt, :], bank[6 + tt][:], out_scale, x1[:, par, tt, :],
                                         ALU.mult, ALU.add).then_inc(S["out_ready"], 1)

            def ffn(f, par, m):
                if m < 2:
                    outputs(f, par, DS - 2 + m)
                if m == 0 and par == 0:
                    save(f, DS - 1)
                if m == 1:
                    finish(f, par)
                if m == 4:
                    low_x(f)
                if m > GU0 and m - GU0 - 1 < JT:
                    gate(f, m - GU0 - 1)
                if m in (DS + 5, DS + 6):
                    result(f, par, m - DS - 5)

            def chunk(c, par, ssm=True, prev=True, rest=True):
                for n in range(DS):
                    if ssm:
                        scans(c, par, n)
                        if n >= 2:
                            outputs(c, par, n - 2)
                        if n and par == 0:
                            save(c, n - 1)
                    if prev:
                        ffn(c - 1, 1 - par, n)
                    if rest:
                        ffn(c - 2, par, DS + n)

            chunk(0, 0, prev=False, rest=False)
            chunk(1, 1, rest=False)
            with dve.Fori(1, NCH // 2) as p:
                for par in range(2):
                    chunk(p * 2 + par, par)
            chunk(NCH, 0, ssm=False)
            chunk(NCH + 1, 1, ssm=False, prev=False)

        @block.tensor
        def _(pe):

            def in_proj(b, et):
                if not isinstance(b, int) or b:
                    after(pe, S["xpad_ready"], b * ET + max(et - 1, 0))
                if et < 2:
                    after(pe, S["eexp_ready"], b * ET)
                    after(pe, S["erelu_ready"], b * ET)
                for k in range(KM):
                    m = pe.matmul(proj_bank(b, et)[:], win_sb[:, k, et * P:(et + 1) * P], ctx_sb[:, k, :],
                                  start=(k == 0), stop=(k == KM - 1))
                m.then_inc(S["xp_ready"], 1)

            def conv(b, et):
                pe.wait_ge(S["xpad_ready"], b * ET + et + 1)
                after(pe, S["vhalf_ready"], b * (2 * ET))
                if et == 2:
                    after(pe, S["xdbl_sb_ready"], b)
                if et == 3:
                    after(pe, S["ct_ready"], b)
                for k in range(KC):
                    m = pe.matmul(bank[2 + et][:], conv_diag[:, et, k, :], xpad[:, et, k:k + L],
                                  start=(k == 0), stop=(k == KC - 1))
                m.then_inc(S["v_ready"], 1)

            def low_rank(b):
                pe.wait_ge(S["vhalf_ready"], b * (2 * ET) + 6)
                for et in range(ET):
                    pe.wait_ge(S["u_ready"], b * ET + et + 1)
                    m = pe.matmul(bank[4][0:NX, :], xproj_sb[:, et, :], u_sb[:, et, :],
                                  start=(et == 0), stop=(et == ET - 1))
                m.then_inc(S["xdbl_ready"], 1)
                pe.wait_ge(S["xdbl_sb_ready"], b + 1)
                for et in range(ET):
                    if et >= 2:
                        pe.wait_ge(S["eexp_ready"], b * ET + et - 1)
                        pe.wait_ge(S["erelu_ready"], b * ET + et - 1)
                    else:
                        pe.wait_ge(S["xpad_ready"], b * ET + ET)
                    pe.matmul(bank[et % 2][:], dt_sb[:, et * P:(et + 1) * P], xdbl_sb[0:DR, :],
                              start=True, stop=True).then_inc(S["dt_ready"], 1)
                after(pe, S["ct_ready"], b)
                settled(pe, S["passed_pe"])
                for tt in range(LT):
                    m = pe.transpose(bank[5][:, tt * NX:(tt + 1) * NX], xdbl_sb[:, tt * P:(tt + 1) * P],
                                     ident[0:NX, 0:NX])
                m.then_inc(S["ctt_ready"], 1)

            def skip_part(b, tt):
                if tt < 2:
                    after(pe, S["gz_st_ready"], b * LT)
                else:
                    pe.wait_ge(S["ud_free"], b * LT + tt - 1)
                for et in range(ET):
                    m = pe.matmul(bank[6 + tt % 2][:, et * P:(et + 1) * P], u_sb[:, et, tt * P:(tt + 1) * P],
                                  d_diag[:, et, :], start=True, stop=True)
                m.then_inc(S["ud_ready"], 1)

            def gate_part(b, st):
                pe.wait_ge(S["gz_ready"], b * LT + st + 1)
                if st < 2:
                    pe.wait_ge(S["ud_free"], b * LT + st + 3)
                else:
                    pe.wait_ge(S["gz_st_ready"], b * LT + st - 1)
                for lt in range(LT):
                    m = pe.transpose(bank[6 + st % 2][:, lt * P:(lt + 1) * P], zn[:, st, lt * P:(lt + 1) * P],
                                     ident[:])
                m.then_inc(S["gzt_ready"], 1)

            def batch(b, last=False):
                low_rank(b)
                for tt in range(LT):
                    skip_part(b, tt)
                if not last:
                    pe.wait_ge(S["ctx_loaded"], b * 16 + 32)
                    in_proj(b + 1, 0)
                    in_proj(b + 1, 1)
                    in_proj(b + 1, 2)
                    in_proj(b + 1, 3)
                gate_part(b, 0)
                gate_part(b, 1)
                if not last:
                    conv(b + 1, 0)
                    conv(b + 1, 1)
                gate_part(b, 2)
                gate_part(b, 3)
                if not last:
                    conv(b + 1, 2)
                    conv(b + 1, 3)

            pe.wait_ge(S["ctx_loaded"], 16)
            pe.wait_ge(S["win_loaded"], 16)
            for et in range(ET):
                in_proj(0, et)
            pe.wait_ge(S["setup"], 1 + ET * (KC + 1))
            for et in range(ET):
                conv(0, et)
            pe.wait_ge(S["params_loaded"], 32)
            pe.wait_ge(S["ident_ready"], 1)
            batch(0)
            with pe.Fori(1, NB - 1) as b:
                batch(b)
            batch(NB - 1, last=True)

            pe.wait_ge(S["ud_free"], NB * LT)
            pe.wait_ge(S["gz_st_ready"], NB * LT)
            pe.wait_ge(S["ct_ready"], NB)
            pe.wait_ge(S["eexp_ready"], NB * ET)
            pe.wait_ge(S["gzt_ready"], NB * LT)
            pe.sem_inc(S["phase_a"], 1)
            pe.wait_ge(S["phase_a"], 4)

            def turn(c, n):
                for tt in range(CT):
                    after(pe, S["stt_done"], c * (DS * CT) + (n - 2) * CT + tt + 1)
                    for et in range(ET):
                        if tt == 0:
                            pe.wait_ge(S["scan_done"], c * (DS * ET) + n * ET + et + 1)
                        m = pe.transpose(bank[2 * (n % 2) + tt][:, et * P:(et + 1) * P],
                                         h[:, n % SLOTS, et, tt * P:(tt + 1) * P], ident[:])
                    m.then_inc(S["ht_ready"], 1)

            def turn_x(f):
                for k in range(2):
                    after(pe, S["q_ready"], f * JT)
                    after(pe, S["us_ready"], f * JT)
                    pe.wait_ge(S["xn_ready"], f * CT + CT)
                    for a in range(2):
                        for tt in range(CT):
                            kt = 2 * k + a
                            m = pe.transpose(bank[4 + k][:, a * TC + tt * P:a * TC + (tt + 1) * P],
                                             xn[:, tt, kt * P:(kt + 1) * P], ident[:])
                    m.then_inc(S["xnt_ready"], 1)

            def gate_up(f, j):
                r = rows(j)
                if j == 0:
                    pe.wait_ge(S["xlo_ready"], f * 2 + 2)
                else:
                    after(pe, S["q_ready"], f * JT + j - 1)
                    after(pe, S["us_ready"], f * JT + j - 1)
                for part, w0 in ((0, 0), (TC, UP0)):
                    i = 0
                    for kt in range(KT):
                        cols = slice(w0 + kt * INTER + j * P, w0 + kt * INTER + j * P + r)
                        for w, v in ((w_hi, xt_hi), (w_hi, xt_lo), (w_lo, xt_hi)):
                            m = pe.matmul(bank[4 + j % 2][0:r, part:part + TC], w[:, cols], v[:, kt, :],
                                          start=(i == 0), stop=(i == 3 * KT - 1))
                            i += 1
                m.then_inc(S["gu_ready"], 1)

            def down(f, part):
                for tt, j in down_parts[part]:
                    r = rows(j)
                    if j % 2 == 0 and tt == 0:
                        pe.wait_ge(S["hlo_ready"], f * 6 + j // 2 + 1)
                    if j == 0:
                        pe.wait_ge(S["out_ready"], f * CT + tt + 1)
                    cols = slice(DN0 + j * HID, DN0 + (j + 1) * HID)
                    toks = slice(tt * P, (tt + 1) * P)
                    for i, (v, w) in enumerate(((h_hi, w_hi), (h_hi, w_lo), (h_lo, w_hi))):
                        m = pe.matmul(bank[6 + tt][:], v[0:r, j, toks], w[0:r, cols],
                                      start=(j == 0 and i == 0), stop=(j == JT - 1 and i == 2))
                    if j == JT - 1:
                        m.then_inc(S["dn_ready"], 1)

            def chunk(c, ssm=True, prev=True, rest=True):
                for n in range(DS):
                    if rest and n < len(down_parts):
                        down(c - 2, n)
                    if prev and n >= GU0:
                        gate_up(c - 1, n - GU0)
                    if prev and n == 3:
                        turn_x(c - 1)
                    if ssm:
                        turn(c, n)

            chunk(0, prev=False, rest=False)
            chunk(1, rest=False)
            with pe.Fori(1, NCH // 2) as p:
                for par in range(2):
                    chunk(p * 2 + par)
            chunk(NCH, ssm=False)
            chunk(NCH + 1, ssm=False, prev=False)


def kernel(x, ctx_1024, L0_xattn_in_proj_w, L0_xattn_conv_w, L0_xattn_conv_b, L0_xattn_x_proj_w,
           L0_xattn_dt_proj_w, L0_xattn_dt_proj_b, L0_xattn_A_log, L0_xattn_D, L0_ffn_lut,
           L0_ffn_gate_idx, L0_ffn_up_idx, L0_ffn_down_idx):
    import numpy as np
    import concourse.bacc as bacc
    from concourse.bass_utils import run_bass_kernel_spmd

    part = 128

    def tiles(a):
        a = np.asarray(a)
        n = -(-a.shape[0] // part)
        full = np.zeros((n * part, a.shape[1]), a.dtype)
        full[:a.shape[0]] = a
        return full.reshape(n, part, a.shape[1]).transpose(1, 0, 2).reshape(part, -1)

    def lay(a):
        return np.ascontiguousarray(np.asarray(a))

    arrays = {
        "ctx_t": lay(np.asarray(ctx_1024).transpose(0, 2, 1)),
        "x": lay(x),
        "win_t": lay(np.asarray(L0_xattn_in_proj_w).T),
        "conv_w": lay(L0_xattn_conv_w),
        "conv_b": lay(L0_xattn_conv_b),
        "xproj_t": lay(np.asarray(L0_xattn_x_proj_w).T),
        "dt_t": lay(np.asarray(L0_xattn_dt_proj_w).T),
        "dt_b": lay(L0_xattn_dt_proj_b),
        "a_log": lay(L0_xattn_A_log),
        "d_skip": lay(L0_xattn_D),
        "lut": lay(L0_ffn_lut),
        "idx": lay(np.concatenate([tiles(np.asarray(L0_ffn_gate_idx).T), tiles(np.asarray(L0_ffn_up_idx).T),
                                   tiles(np.asarray(L0_ffn_down_idx).T)], axis=1)),
    }
    nc = bacc.Bacc("TRN2", target_bir_lowering=False, num_devices=1)
    args = [nc.dram_tensor(f"in_{k}", a.shape, mybir.dt.from_np(a.dtype), kind="ExternalInput").ap()
            for k, a in arrays.items()]
    out = nc.dram_tensor("out_0", arrays["x"].shape, F32, kind="ExternalOutput").ap()
    mamba_ffn(nc, *args, out)
    r = run_bass_kernel_spmd(nc, [{f"in_{k}": a for k, a in arrays.items()}], core_ids=[0])
    return r.results[0]["out_0"]
```
